# Optimizing a Trainium2 kernel written in Bass

```python
import numpy as np
import jax
import jax.numpy as jnp

def _softmax(x, axis=-1):
    return jax.nn.softmax(x, axis=axis)
def _gelu(x):
    return jax.nn.gelu(x, approximate=True)
def _silu(x):
    return jax.nn.silu(x)
def _sigmoid(x):
    return jax.nn.sigmoid(x)
def _layernorm(x, axis=-1, eps=1e-5):
    m = jnp.mean(x, axis=axis, keepdims=True)
    v = jnp.var(x, axis=axis, keepdims=True)
    return (x - m) / jnp.sqrt(v + eps)
def _scatter_add(tgt, idx, src, axis=0):
    return tgt.at[idx].add(src)
def _segment_sum(src, seg, n):
    return jax.ops.segment_sum(src, seg, n)

kernel_name = 'mk_adj_preln_d2_adj_512_f8782f'

def setup_inputs(seed: int = 0):
    np.random.seed(seed)
    _w = jnp.asarray
    def _rec_inputs():
        import jax
        import jax.numpy as jnp
        _gk = jax.random.key(seed)
        x = -0.0005207 + 1.001 * jax.random.normal(jax.random.fold_in(_gk, 1), (4096, 512), jnp.float32)
        _a = jax.random.bernoulli(jax.random.fold_in(_gk, 2), 0.000976562, (4096, 4096))
        _a = jnp.logical_or(_a, jnp.swapaxes(_a, -1, -2))
        _a = jnp.logical_or(_a, jnp.eye(4096, dtype=bool))
        adj = _a.astype(jnp.int32)
        return x, adj
    x, adj = _rec_inputs()
    def _L0_gnn_setup():
        import jax, jax.numpy as jnp
        import numpy as np
        N = 4096
        IN_FEAT = 512
        EMBED = 512
        HEADS = 8
        HEAD_DIM = EMBED // HEADS
        SCALING = HEAD_DIM ** (-0.5)
        key = jax.random.key(seed)
        ks = jax.random.split(key, 7)
        x = jax.random.normal(ks[0], (N, IN_FEAT), dtype=jnp.float32)
        adj = jax.random.randint(ks[1], (N, N), 0, 2, dtype=jnp.int32)
        s = 0.04
        WQ = jax.random.normal(ks[2], (EMBED, IN_FEAT), dtype=jnp.float32) * s
        WK = jax.random.normal(ks[3], (EMBED, IN_FEAT), dtype=jnp.float32) * s
        WV = jax.random.normal(ks[4], (EMBED, IN_FEAT), dtype=jnp.float32) * s
        we = jax.random.normal(ks[5], (1, HEAD_DIM), dtype=jnp.float32) * 0.1
        be = jnp.zeros((1,), dtype=jnp.float32)
        return {'x': x, 'adj': adj, 'WQ': WQ, 'WK': WK, 'WV': WV, 'we': we, 'be': be}
    _L0_gnn_all = _L0_gnn_setup()
    _L0_gnn_in = {k: v for k, v in _L0_gnn_all.items() if k in ('WQ', 'WK', 'WV', 'we', 'be', )}
    del _L0_gnn_all

    def _L1_gnn_setup():
        import jax, jax.numpy as jnp
        import numpy as np
        N, D_IN, D_OUT = (8192, 512, 512)
        key = jax.random.key(seed)
        ks = jax.random.split(key, 8)
        scale_in = 1.0 / np.sqrt(D_IN)
        scale_cat = 1.0 / np.sqrt(2 * D_OUT)
        return {'x': jax.random.normal(ks[0], (N, D_IN), dtype=jnp.float32), 'adj': jax.random.randint(ks[1], (N, N), 0, 2, dtype=jnp.int32), 'W_self': jax.random.uniform(ks[2], (D_IN, D_OUT), jnp.float32, -scale_in, scale_in), 'b_self': jax.random.uniform(ks[3], (D_OUT,), jnp.float32, -scale_in, scale_in), 'W_nb': jax.random.uniform(ks[4], (D_IN, D_OUT), jnp.float32, -scale_in, scale_in), 'b_nb': jax.random.uniform(ks[5], (D_OUT,), jnp.float32, -scale_in, scale_in), 'W_comb': jax.random.uniform(ks[6], (2 * D_OUT, D_OUT), jnp.float32, -scale_cat, scale_cat), 'b_comb': jax.random.uniform(ks[7], (D_OUT,), jnp.float32, -scale_cat, scale_cat)}
    _L1_gnn_all = _L1_gnn_setup()
    _L1_gnn_in = {k: v for k, v in _L1_gnn_all.items() if k in ('W_self', 'b_self', 'W_nb', 'b_nb', 'W_comb', 'b_comb', )}
    del _L1_gnn_all

    return {
        "x": x,
        "adj": adj,
        "L0_gnn_WQ": _L0_gnn_in["WQ"],
        "L0_gnn_WK": _L0_gnn_in["WK"],
        "L0_gnn_WV": _L0_gnn_in["WV"],
        "L0_gnn_we": _L0_gnn_in["we"],
        "L0_gnn_be": _L0_gnn_in["be"],
        "L1_gnn_W_self": _L1_gnn_in["W_self"],
        "L1_gnn_b_self": _L1_gnn_in["b_self"],
        "L1_gnn_W_nb": _L1_gnn_in["W_nb"],
        "L1_gnn_b_nb": _L1_gnn_in["b_nb"],
        "L1_gnn_W_comb": _L1_gnn_in["W_comb"],
        "L1_gnn_b_comb": _L1_gnn_in["b_comb"],
    }

def reference(x, adj, L0_gnn_WQ, L0_gnn_WK, L0_gnn_WV, L0_gnn_we, L0_gnn_be, L1_gnn_W_self, L1_gnn_b_self, L1_gnn_W_nb, L1_gnn_b_nb, L1_gnn_W_comb, L1_gnn_b_comb):
    import jax
    import jax.numpy as jnp
    def _L0_gnn_ref(x, adj, WQ, WK, WV, we, be):
        import jax, jax.numpy as jnp
        import numpy as np
        N = 4096
        IN_FEAT = 512
        EMBED = 512
        HEADS = 8
        HEAD_DIM = EMBED // HEADS
        SCALING = HEAD_DIM ** (-0.5)
        n = x.shape[0]
        Q = (x @ WQ.T).reshape(n, HEADS, HEAD_DIM).transpose(1, 0, 2)
        K = (x @ WK.T).reshape(n, HEADS, HEAD_DIM).transpose(1, 0, 2)
        V = (x @ WV.T).reshape(n, HEADS, HEAD_DIM).transpose(1, 0, 2)
        energy = Q @ we.T + be
        attn = jnp.einsum('hqd,hkd->hqk', Q, K) * SCALING + energy
        attn = attn + jnp.where(adj > 0, 0.0, -jnp.inf)
        attn = jax.nn.softmax(attn, axis=-1)
        hard = (attn == jnp.max(attn, axis=-1, keepdims=True)).astype(jnp.float32) / HEADS
        out = jnp.einsum('hqk,hkd->hqd', hard, V)
        return out.transpose(1, 0, 2).reshape(n, EMBED)

    def _L1_gnn_ref(x, adj, W_self, b_self, W_nb, b_nb, W_comb, b_comb):
        import jax, jax.numpy as jnp
        import numpy as np
        N, D_IN, D_OUT = (8192, 512, 512)
        mask = (adj > 0).astype(x.dtype)
        deg = jnp.sum(mask, axis=1, keepdims=True)
        agg = mask @ x / jnp.maximum(deg, 1.0)
        self_f = x @ W_self + b_self
        nb_f = agg @ W_nb + b_nb
        combined = jnp.concatenate([self_f, nb_f], axis=-1)
        out = combined @ W_comb + b_comb
        return jax.nn.relu(out)

    h = jnp.maximum(_layernorm(x, axis=-1), 0.0)
    x = x + _L0_gnn_ref(h, adj, L0_gnn_WQ, L0_gnn_WK, L0_gnn_WV, L0_gnn_we, L0_gnn_be)
    h = jnp.maximum(_layernorm(x, axis=-1), 0.0)
    x = x + _L1_gnn_ref(h, adj, L1_gnn_W_self, L1_gnn_b_self, L1_gnn_W_nb, L1_gnn_b_nb, L1_gnn_W_comb, L1_gnn_b_comb)
    return x


_drawn_inputs = setup_inputs


def setup_inputs(seed=0):
    import zlib

    import numpy as np

    out = dict(_drawn_inputs(seed))
    spreads = {}
    factors = {'L1_gnn_b_self': 8.0, 'L1_gnn_b_nb': 7.842, 'L1_gnn_b_comb': 4.748}
    for name, (base, spread) in spreads.items():
        noise = np.random.default_rng([zlib.crc32(name.encode()), seed]).standard_normal(out[name].shape)
        drawn = base * np.exp(spread * noise) if base else spread * noise
        out[name] = jnp.asarray(drawn.astype(out[name].dtype))
    for name, factor in factors.items():
        out[name] = (out[name] * factor).astype(out[name].dtype)
    return out
```

```python
from contextlib import ExitStack

import concourse.bass as bass
from concourse import mybir

F32 = mybir.dt.float32
BF16 = mybir.dt.bfloat16
I8 = mybir.dt.int8
I32 = mybir.dt.int32
ALU = mybir.AluOpType
ACT = mybir.ActivationFunctionType

P = 128
N = 4096
D = 512
HEADS = 8
HD = D // HEADS
KC = D // P
TILES = N // P
GT = 4
GROUPS = TILES // GT
GR = GT * P
PARTS = 3
BLOCKS = N // (2 * P)
EPS = 1e-5
SCALING = HD ** -0.5
HH = 4
HALF = HH * HD
SC = 1024
CHUNKS = N // SC
TB = BLOCKS // CHUNKS
MASKED = -1e30
FLOOR = -1e29
TIE = 2.0 ** -25


class Steps:

    def __init__(self, engine, sem):
        self.engine, self.sem, self.base, self.n = engine, sem, 0, 0

    def turn(self, base):
        self.base, self.n = base, 0

    def done(self, instruction):
        self.n += 1
        instruction.then_inc(self.sem, 1)
        self.engine.wait_ge(self.sem, self.base + self.n)


class Gate:

    def __init__(self, engine, sem):
        self.engine, self.sem = engine, sem

    def wait_ge(self, sem, value):
        self.engine.wait_ge(sem, value)
        self.engine.sem_inc(self.sem, 1)


def make_identity(nc, pool, ident, sem):
    nc.gpsimd.memset(ident[:], 0.0).then_inc(sem, 1)
    pool.wait_ge(sem, 1)
    nc.gpsimd.affine_select(out=ident[:], in_=ident[:], compare_op=ALU.not_equal, fill=1.0, base=0,
                            pattern=[[-1, P]], channel_multiplier=1).then_inc(sem, 1)


NORM_STEPS = 2 * GT + 7


def normalise(nc, v, gate, steps, x, xn, stats, mv, small, var_ready, root_ready, turn):
    for t in range(GT):
        nc.vector.bn_stats(stats[:, t, :], x[:, t, :]).then_inc(steps.sem, 1)
        steps.n += 1
    gate.wait_ge(steps.sem, steps.base + steps.n)
    for t in range(GT):
        nc.vector.bn_aggr(mv[:, t, :], stats[:, t, :]).then_inc(steps.sem, 1)
        steps.n += 1
    v.wait_ge(steps.sem, steps.base + steps.n)
    var, root, inv, other = (small[:, i, :] for i in range(4))
    nc.vector.tensor_scalar(var, mv[:, :, 1], EPS, None, ALU.add).then_inc(var_ready, 1)
    v.wait_ge(root_ready, turn + 1)
    steps.done(nc.vector.reciprocal(inv, root))
    steps.done(nc.vector.tensor_tensor(other, var, inv, ALU.mult))
    steps.done(nc.vector.tensor_tensor(other, other, root, ALU.add))
    steps.done(nc.vector.tensor_scalar(other, other, 0.5, None, ALU.mult))
    steps.done(nc.vector.reciprocal(inv, other))
    for t in range(GT):
        last = nc.vector.tensor_scalar(xn[:, t, :], x[:, t, :], mv[:, t, 0:1], inv[:, t:t + 1],
                                       ALU.subtract, ALU.mult)
    return last


SPLIT_STEPS = 3


def split(nc, steps, value, rest, high, middle, low):
    steps.done(nc.vector.tensor_copy(high, value))
    steps.done(nc.vector.tensor_tensor(rest, value, high, ALU.subtract))
    steps.done(nc.vector.tensor_copy(middle, rest))
    return nc.vector.tensor_tensor(low, rest, middle, ALU.subtract)


def projections(nc, sem, x, adj, WQ, WK, WV, we, q_scr, k_scr, v_scr, sign_scr):
    x_v = x.rearrange("(g t p) f -> g p t f", t=GT, p=P)
    adj_v = adj.rearrange("(t p) k -> t p k", p=P)
    v_v = v_scr.rearrange("(g t p) c f -> g p t c f", t=GT, p=P)
    UN = 2
    OUTS = 3 * KC
    NEXT_AT = 7

    with ExitStack() as ctx:
        def sb(name, shape, dt):
            return ctx.enter_context(nc.sbuf_tensor(name, shape, dt))

        ident = sb("p_ident", [P, P], F32)
        w_rows = sb("p_w_rows", [P, 3, KC, D], F32)
        wT = sb("p_wT", [P, 3, KC, D], F32)
        we_col = sb("p_we_col", [P, 1], F32)
        xb = sb("p_x", [P, UN, GT, D], F32)
        xn = sb("p_xn", [P, GT, D], F32)
        hT = sb("p_hT", [P, UN, KC, GR], F32)
        stats = sb("p_stats", [P, GT, 6], F32)
        mv = sb("p_mv", [P, GT, 2], F32)
        small = sb("p_small", [P, 4, GT], F32)
        value = sb("p_value", [P, 2, D], F32)
        rest = sb("p_rest", [P, D], F32)
        k_parts = sb("p_k_parts", [P, PARTS, KC, GR], BF16)
        q_parts = sb("p_q_parts", [P, PARTS, KC, GR], BF16)
        v_parts = sb("p_v_parts", [P, GT, PARTS, D], BF16)
        adj_rows = sb("p_adj", [P, 2, N // 2], I32)
        signs = sb("p_signs", [P, 2, N // 2], I8)
        ps_t = ctx.enter_context(nc.psum_tensor("p_ps_t", [P, 2, D], F32))
        ps_o = ctx.enter_context(nc.psum_tensor("p_ps_o", [P, 4, D], F32))

        w_loaded = sem("p_w_loaded")
        ident_ready = sem("p_ident_ready")
        x_loaded = [sem(f"p_x_loaded{u}") for u in range(UN)]
        adj_loaded = [sem(f"p_adj_loaded{u}") for u in range(2)]
        signs_ready = sem("p_signs_ready")
        signs_stored = [sem(f"p_signs_stored{u}") for u in range(2)]
        var_ready = sem("p_var_ready")
        root_ready = sem("p_root_ready")
        xn_ready = sem("p_xn_ready")
        rows_turned = sem("p_rows_turned")
        turned_kept = sem("p_turned_kept")
        out_ready = sem("p_out_ready")
        value_ready = sem("p_value_ready")
        value_split = sem("p_value_split")
        dve_step = sem("p_dve_step")
        k_stored = sem("p_k_stored")
        q_stored = sem("p_q_stored")
        v_stored = sem("p_v_stored")
        sp_passed = sem("p_sp_passed")
        dve_passed = sem("p_dve_passed")
        block = ctx.enter_context(nc.Block())

        W_FILLS = 3 * KC
        HALVES = 2 * GT

        @block.gpsimd
        def _(pool):
            make_identity(nc, pool, ident, ident_ready)

        @block.sync
        def _(sp):
            sp_gate = Gate(sp, sp_passed)
            for i, w in enumerate((WK, WQ, WV)):
                sp.dma_start(w_rows[:, i, :, :], w.rearrange("(c p) f -> p c f", p=P)).then_inc(w_loaded, 16)
            for a in range(2):
                sp.dma_start(we_col[a * HD:(a + 1) * HD, :], we.rearrange("a d -> d a")).then_inc(w_loaded, 16)
            for u in range(UN):
                sp.dma_start(xb[:, u, :, :], x_v[u, :, :, :]).then_inc(x_loaded[u], 16)

            def load_adj(tile, a, count):
                sp.dma_start(adj_rows[:, a, :], adj_v[tile, :, a * N // 2:(a + 1) * N // 2])\
                  .then_inc(adj_loaded[a], 16)

            def store_signs(tile, a, count):
                sp_gate.wait_ge(signs_ready, count + 1)
                sp.dma_start(sign_scr[tile, :, a * N // 2:(a + 1) * N // 2], signs[:, a, :])\
                  .then_inc(signs_stored[a], 16)

            for a in range(2):
                sp.sem_inc(signs_stored[a], 16)
                load_adj(0, a, a)

            def group(g, u, last, last_x):
                for t in range(GT):
                    for a in range(2):
                        store_signs(g * GT + t, a, g * HALVES + (2 * t + a))
                        if not (last and t == GT - 1):
                            load_adj(g * GT + (t + 1), a, g * HALVES + (2 * t + a))
                    if t == 1:
                        sp_gate.wait_ge(value_split, g * OUTS + (2 + KC))
                        for stack, (upper, lower) in enumerate(((0, 1), (2, 0))):
                            for at, part in ((0, upper), (HD, lower)):
                                for a in range(2):
                                    sp.dma_start(
                                        k_scr[a::2, stack, at:at + HD, bass.ts(g, GR)].rearrange("c p r -> p c r"),
                                        k_parts[a * HD:(a + 1) * HD, part, :, :]).then_inc(k_stored, 16)
                    if t == 2:
                        sp_gate.wait_ge(value_split, g * OUTS + (2 + 2 * KC))
                        for stack, (upper, lower) in enumerate(((0, 0), (1, 1), (0, 2))):
                            for at, part in ((0, upper), (HD, lower)):
                                for a in range(2):
                                    sp.dma_start(
                                        q_scr[a::2, stack, at:at + HD, bass.ts(g, GR)].rearrange("c p r -> p c r"),
                                        q_parts[a * HD:(a + 1) * HD, part, :, :]).then_inc(q_stored, 16)
                    if t == 3:
                        if not last_x:
                            sp_gate.wait_ge(xn_ready, g + 1)
                            sp.dma_start(xb[:, u, :, :], x_v[g + 2, :, :, :]).then_inc(x_loaded[u], 16)
                        sp_gate.wait_ge(value_split, g * OUTS + (2 + 3 * KC))
                        for i in range(GT):
                            sp.dma_start(v_v[g, :, i, :, :], v_parts[:, i, :, :]).then_inc(v_stored, 16)

            with sp.Fori(0, GROUPS // UN - 1) as it:
                for u in range(UN):
                    group(it * UN + u, u, False, False)
            for u in range(UN):
                group(GROUPS - UN + u, u, u == UN - 1, True)
            sp_gate.wait_ge(k_stored, GROUPS * 8 * 16)
            sp_gate.wait_ge(q_stored, GROUPS * 12 * 16)
            sp_gate.wait_ge(v_stored, GROUPS * GT * 16)
            for a in range(2):
                sp_gate.wait_ge(signs_stored[a], TILES * 16 + 16)

        @block.tensor
        def _(pe):
            pe.wait_ge(ident_ready, 2)
            pe.wait_ge(w_loaded, 5 * 16)
            for f in range(W_FILLS):
                i, k = f // KC, f % KC
                pe.wait_ge(turned_kept, f + 1)
                for c in range(KC):
                    last = nc.tensor.transpose(ps_t[:, f % 2, c * P:(c + 1) * P],
                                               w_rows[:, i, c, k * P:(k + 1) * P], ident[:])
                last.then_inc(rows_turned, 1)

            def turn_rows(g):
                pe.wait_ge(xn_ready, g + 1)
                for k in range(KC):
                    pe.wait_ge(turned_kept, g * KC + (W_FILLS + k + 1))
                    for t in range(GT):
                        last = nc.tensor.transpose(ps_t[:, k % 2, t * P:(t + 1) * P],
                                                   xn[:, t, k * P:(k + 1) * P], ident[:])
                    last.then_inc(rows_turned, 1)

            def group(g, u, last_group):
                pe.wait_ge(turned_kept, g * KC + (W_FILLS + KC + 2))
                for o in range(OUTS):
                    pe.wait_ge(value_ready, g * OUTS + (o + 1))
                    i, c = o // KC, o % KC
                    for k in range(KC):
                        if i < 2:
                            lhsT, rhs = wT[:, i, k, c * P:(c + 1) * P], hT[:, u, k, :]
                        else:
                            lhsT, rhs = hT[:, u, k, c * P:(c + 1) * P], wT[:, i, k, :]
                        last = nc.tensor.matmul(ps_o[:, o % 4, :], lhsT, rhs, start=k == 0, stop=k == KC - 1)
                    last.then_inc(out_ready, 1)
                    if o == NEXT_AT and not last_group:
                        turn_rows(g + 1)

            turn_rows(0)
            with pe.Fori(0, GROUPS // UN - 1) as it:
                for u in range(UN):
                    group(it * UN + u, u, False)
            for u in range(UN):
                group(GROUPS - UN + u, u, u == UN - 1)

        @block.scalar
        def _(act):
            act.sem_inc(turned_kept, 2)
            act.sem_inc(value_ready, 4)
            for f in range(W_FILLS):
                act.wait_ge(rows_turned, f + 1)
                nc.scalar.copy(wT[:, f // KC, f % KC, :], ps_t[:, f % 2, :]).then_inc(turned_kept, 1)
            act.wait_ge(w_loaded, 5 * 16)

            def root(g):
                act.wait_ge(var_ready, g + 1)
                nc.scalar.activation(small[:, 1, :], small[:, 0, :], ACT.Sqrt).then_inc(root_ready, 1)

            def keep_rows(g, u):
                for k in range(KC):
                    act.wait_ge(rows_turned, g * KC + (W_FILLS + k + 1))
                    nc.scalar.activation(hT[:, u, k, :], ps_t[:, k % 2, :], ACT.Relu).then_inc(turned_kept, 1)

            def sign(a, count, tile):
                act.wait_ge(adj_loaded[a], tile * 16 + 16)
                act.wait_ge(signs_stored[a], tile * 16 + 16)
                nc.scalar.activation(signs[:, a, :], adj_rows[:, a, :], ACT.Sign).then_inc(signs_ready, 1)

            def group(g, u, last_group):
                for o in range(OUTS):
                    if o < HALVES:
                        sign(o % 2, g * HALVES + o, g * GT + o // 2)
                    if o == 7 and not last_group:
                        root(g + 1)
                    act.wait_ge(out_ready, g * OUTS + (o + 1))
                    act.wait_ge(value_split, g * OUTS + (o + 1))
                    if o < KC:
                        nc.scalar.activation(value[:, o % 2, :], ps_o[:, o % 4, :], ACT.Identity,
                                             bias=we_col[:, 0:1], scale=SCALING).then_inc(value_ready, 1)
                    else:
                        nc.scalar.copy(value[:, o % 2, :], ps_o[:, o % 4, :]).then_inc(value_ready, 1)
                    if o == NEXT_AT and not last_group:
                        keep_rows(g + 1, 1 - u)

            root(0)
            keep_rows(0, 0)
            with act.Fori(0, GROUPS // UN - 1) as it:
                for u in range(UN):
                    group(it * UN + u, u, False)
            for u in range(UN):
                group(GROUPS - UN + u, u, u == UN - 1)

        @block.vector
        def _(v):
            v.sem_inc(value_split, 2)
            steps = Steps(v, dve_step)
            NORM = NORM_STEPS - 2
            PER = OUTS * SPLIT_STEPS + NORM

            def norm(g, u, it):
                v.wait_ge(x_loaded[u], it * 16 + 16)
                if not isinstance(g, int) or g > 0:
                    v.wait_ge(turned_kept, g * KC + (W_FILLS + 2))
                normalise(nc, v, Gate(v, dve_passed), steps, xb[:, u], xn, stats, mv, small, var_ready, root_ready, g)\
                    .then_inc(xn_ready, 1)

            def group(g, u, it, last_group):
                steps.turn(g * PER + NORM)
                for o in range(OUTS):
                    i, c = o // KC, o % KC
                    v.wait_ge(value_ready, g * OUTS + (o + 5))
                    if not isinstance(g, int) or g > 0:
                        if o == 0:
                            v.wait_ge(k_stored, g * (8 * 16))
                        if o == KC:
                            v.wait_ge(q_stored, g * (12 * 16))
                        if o == 2 * KC:
                            v.wait_ge(v_stored, g * (GT * 16))
                    parts = [(k_parts[:, n, c, :], q_parts[:, n, c, :], v_parts[:, c, n, :])[i] for n in range(PARTS)]
                    split(nc, steps, value[:, o % 2, :], rest[:], *parts).then_inc(value_split, 1)
                    if o == 5 and not last_group:
                        norm(g + 1, 1 - u, it + u)

            steps.turn(0)
            norm(0, 0, 0)
            assert steps.n == NORM, steps.n
            group(0, 0, 0, False)
            assert steps.n == PER, steps.n
            group(1, 1, 0, False)
            with v.Fori(1, GROUPS // UN - 1) as it:
                for u in range(UN):
                    group(it * UN + u, u, it, False)
            for u in range(UN):
                group(GROUPS - UN + u, u, GROUPS // UN - 1, u == UN - 1)


def attention(nc, sem, half, x, be, q_scr, k_scr, v_scr, sign_scr, x1_scr):
    n_ = f"a{half}_"
    h0 = half * HH
    cols = slice(half * HALF, (half + 1) * HALF)
    v_v = v_scr.rearrange("(b j e) c f -> j b e c f", j=P, e=2)
    x_v = x.rearrange("(t p) f -> t p f", p=P)
    x1_v = x1_scr.rearrange("(t p) f -> t p f", p=P)
    UN = 2
    LAG = 2
    TILE_CHUNKS = HH * CHUNKS
    PAIRS = HH // 2

    with ExitStack() as ctx:
        def sb(name, shape, dt):
            return ctx.enter_context(nc.sbuf_tensor(n_ + name, shape, dt))

        ident = sb("ident", [P, P], F32)
        be_col = sb("be", [P, 1], F32)
        k_sb = sb("k", [P, HH, 2, N], BF16)
        v_sb = sb("v", [P, BLOCKS, 2, PARTS, HALF], BF16)
        q_sb = sb("q", [P, UN, HH, 3, P], BF16)
        signs = sb("signs", [P, UN, N], I8)
        bias = sb("bias", [P, UN, N], BF16)
        scores = sb("scores", [P, N], F32)
        top = sb("top", [P, CHUNKS], F32)
        least = sb("least", [P, 1], F32)
        hits = sb("hits", [P, 2, N], BF16)
        hitsT = sb("hitsT", [P, 4, TB, P, 2], BF16)
        xt = sb("xt", [P, UN, HALF], F32)
        picked = sb("picked", [P, 2, 2, PARTS, HD], F32)
        ps_s = ctx.enter_context(nc.psum_tensor(n_ + "ps_s", [P, 2, SC], F32))
        ps_t = ctx.enter_context(nc.psum_tensor(n_ + "ps_t", [P, 2, TB * P], F32))
        ps_o = ctx.enter_context(nc.psum_tensor(n_ + "ps_o", [P, 2, 512], F32))

        ident_ready = sem(n_ + "ident_ready")
        be_loaded = sem(n_ + "be_loaded")
        k_loaded = [sem(n_ + f"k_loaded{h}") for h in range(HH)]
        v_loaded = sem(n_ + "v_loaded")
        q_loaded = [sem(n_ + f"q_loaded{u}") for u in range(UN)]
        signs_loaded = [sem(n_ + f"signs_loaded{u}") for u in range(UN)]
        x_loaded = [sem(n_ + f"x_loaded{u}") for u in range(UN)]
        bias_ready = sem(n_ + "bias_ready")
        scores_ready = sem(n_ + "scores_ready")
        scores_used = sem(n_ + "scores_used")
        dve_step = sem(n_ + "dve_step")
        hits_ready = sem(n_ + "hits_ready")
        hits_turned = sem(n_ + "hits_turned")
        turned_kept = sem(n_ + "turned_kept")
        turned_used = sem(n_ + "turned_used")
        out_ready = sem(n_ + "out_ready")
        picked_ready = sem(n_ + "picked_ready")
        pool_step = sem(n_ + "pool_step")
        pair_added = sem(n_ + "pair_added")
        x1_stored = [sem(n_ + f"x1_stored{u}") for u in range(UN)]
        sp_passed = sem(n_ + "sp_passed")
        dve_passed = sem(n_ + "dve_passed")
        pool_passed = sem(n_ + "pool_passed")
        block = ctx.enter_context(nc.Block())

        @block.sync
        def _(sp):
            sp_gate = Gate(sp, sp_passed)
            sp.dma_start(be_col[:], be.rearrange("(a b) -> a b", a=1).broadcast_to([P, 1])).then_inc(be_loaded, 16)

            def load_k(h):
                sp.dma_start(k_sb[:, h, :, :], k_scr[h0 + h, :, :, :].rearrange("s p n -> p s n"))\
                  .then_inc(k_loaded[h], 16)

            def load_q(t, u):
                sp.dma_start(q_sb[:, u, :, :, :].rearrange("p h s r -> p (h s) r"),
                             q_scr[h0:h0 + HH, :, :, bass.ts(t, P)].rearrange("h s p r -> p (h s) r"))\
                  .then_inc(q_loaded[u], 16)

            def load_signs(t, u):
                sp.dma_start(signs[:, u, :], sign_scr[t, :, :]).then_inc(signs_loaded[u], 16)

            def load_x(t, u):
                sp.dma_start(xt[:, u, :], x_v[t, :, cols]).then_inc(x_loaded[u], 16)

            def store(t, u):
                sp_gate.wait_ge(pair_added, t * PAIRS + (PAIRS + 2))
                sp.dma_start(x1_v[t, :, cols], xt[:, u, :]).then_inc(x1_stored[u], 16)

            load_signs(0, 0)
            load_q(0, 0)
            load_k(0)
            load_k(1)
            load_signs(1, 1)
            for e in range(2):
                for n in range(PARTS):
                    sp.dma_start(v_sb[:, :, e, n, :], v_v[:, :, e, n, cols]).then_inc(v_loaded, 16)
            load_k(2)
            load_x(0, 0)
            load_k(3)
            load_q(1, 1)
            load_x(1, 1)
            with sp.Fori(1, TILES // UN) as it:
                for u in range(UN):
                    t = it * UN + u
                    sp_gate.wait_ge(bias_ready, t - 1)
                    load_signs(t, u)
                    sp_gate.wait_ge(scores_ready, (t - 1) * TILE_CHUNKS)
                    load_q(t, u)
                    store(t - 2, u)
                    sp_gate.wait_ge(x1_stored[u], it * 16)
                    load_x(t, u)
            for u in range(UN):
                store(TILES - UN + u, u)
            for u in range(UN):
                sp_gate.wait_ge(x1_stored[u], TILES // UN * 16)

        @block.gpsimd
        def _(pool):
            make_identity(nc, pool, ident, ident_ready)
            pool.sem_inc(pair_added, 2)
            steps = Steps(pool, pool_step)

            def make_bias(t, u, it):
                pool.wait_ge(signs_loaded[u], it * 16 + 16)
                if not isinstance(t, int) or t > 0:
                    Gate(pool, pool_passed).wait_ge(scores_used, (t - 1) * TILE_CHUNKS + 2)
                nc.gpsimd.tensor_scalar(bias[:, u, :], signs[:, u, :], 0.0, MASKED, ALU.is_le, ALU.mult)\
                  .then_inc(bias_ready, 1)

            def add_pairs(t, u, it):
                pool.wait_ge(x_loaded[u], it * 16 + 16)
                steps.turn(t * (PAIRS * 2))
                for m in range(PAIRS):
                    pool.wait_ge(picked_ready, t * PAIRS + (m + 3))
                    part = [picked[:, m, :, n, :] for n in range(PARTS)]
                    to = xt[:, u, m * P:(m + 1) * P].rearrange("p (a d) -> p a d", a=2)
                    steps.done(nc.gpsimd.tensor_tensor(part[2], part[2], part[1], ALU.add))
                    steps.done(nc.gpsimd.tensor_tensor(part[2], part[2], part[0], ALU.add))
                    nc.gpsimd.tensor_tensor(to, to, part[2], ALU.add).then_inc(pair_added, 1)

            make_bias(0, 0, 0)
            make_bias(1, 1, 0)
            add_pairs(0, 0, 0)
            with pool.Fori(1, TILES // UN) as it:
                make_bias(it * UN, 0, it)
                add_pairs(it * UN - 1, 1, it - 1)
                make_bias(it * UN + 1, 1, it)
                add_pairs(it * UN, 0, it)
            add_pairs(TILES - 1, 1, TILES // UN - 1)

        @block.tensor
        def _(pe):
            pe.sem_inc(turned_used, 4)
            pe.sem_inc(hits_turned, 2 * CHUNKS)
            pe.wait_ge(ident_ready, 2)

            def score_chunk(s, u, h, c, it):
                if c == 0 and h == 0:
                    pe.wait_ge(q_loaded[u], it * 16 + 16)
                if isinstance(s, int) and s < HH and c == 0:
                    pe.wait_ge(k_loaded[s], 16)
                pe.wait_ge(scores_used, s * CHUNKS + (c + 1))
                for n in range(SC // 512):
                    keys = slice(c * SC + n * 512, c * SC + (n + 1) * 512)
                    for i, (qs, ks) in enumerate(((0, 0), (1, 0), (2, 1))):
                        last = nc.tensor.matmul(ps_s[:, c % 2, n * 512:(n + 1) * 512], q_sb[:, u, h, qs, :],
                                                k_sb[:, h, ks, keys], start=i == 0, stop=i == 2)
                last.then_inc(scores_ready, 1)

            def turn_chunk(s, h, c):
                if c == 0:
                    pe.wait_ge(hits_ready, s + 2)
                pe.wait_ge(turned_kept, s * CHUNKS + (c + 1))
                pairs = hits[:, h % 2, :].bitcast(F32)
                for b in range(TB):
                    at = (c * TB + b) * P
                    last = nc.tensor.transpose(ps_t[:, c % 2, b * P:(b + 1) * P], pairs[:, at:at + P], ident[:])
                last.then_inc(hits_turned, 1)

            def value_chunk(s, h, c, pair):
                if isinstance(s, int) and s == 0 and c == 0:
                    pe.wait_ge(v_loaded, 2 * PARTS * 16)
                if c == 0 and h % 2 == 0:
                    pe.wait_ge(picked_ready, pair + 1)
                pe.wait_ge(turned_kept, s * CHUNKS + (c + 3))
                a = h % 2
                to = ps_o[:, (h // 2) % 2, a * PARTS * HD:(a + 1) * PARTS * HD].rearrange("p (c d) -> p c d", c=PARTS)
                for b in range(TB):
                    for e in range(2):
                        last = nc.tensor.matmul(to, hitsT[:, c, b, :, e],
                                                v_sb[:, c * TB + b, e, :, h * HD:(h + 1) * HD],
                                                start=a == 0 and c == 0 and b == 0 and e == 0,
                                                stop=c == CHUNKS - 1 and b == TB - 1 and e == 1,
                                                skip_group_check=True)
                last.then_inc(turned_used, 1)

            def turn(it, j, scored, valued):
                s = it * (UN * HH) + j
                h = j % HH
                sv = s - LAG
                hv = (j - LAG) % HH
                pair = it * (UN * PAIRS) + (j - LAG) // 2
                for c in range(CHUNKS):
                    if valued:
                        turn_chunk(sv, hv, c)
                    if scored:
                        score_chunk(s, j // HH % UN, h, c, it)
                    if valued and c > 0:
                        value_chunk(sv, hv, c - 1, pair)
                if valued:
                    value_chunk(sv, hv, CHUNKS - 1, pair)

            for j in range(UN * HH):
                turn(0, j, True, j >= LAG)
            with pe.Fori(1, TILES // UN) as it:
                for j in range(UN * HH):
                    turn(it, j, True, True)
            for j in range(LAG):
                turn(TILES // UN, j, False, True)

        @block.scalar
        def _(act):
            act.sem_inc(turned_kept, 2)
            act.sem_inc(picked_ready, 2)
            with act.Fori(0, TILES // UN) as it:
                for j in range(UN * HH):
                    s = it * (UN * HH) + j
                    for c in range(CHUNKS):
                        act.wait_ge(hits_turned, s * CHUNKS + (c + 1 + 2 * CHUNKS))
                        act.wait_ge(turned_used, s * CHUNKS + (c + 1))
                        nc.scalar.copy(hitsT[:, c, :, :, :].rearrange("p b q e -> p (b q e)"),
                                       ps_t[:, c % 2, :].bitcast(BF16)).then_inc(turned_kept, 1)
                    if j % 2:
                        pair = it * (UN * PAIRS) + j // 2
                        m = j // 2 % PAIRS
                        act.wait_ge(turned_used, s * CHUNKS + (CHUNKS + 4))
                        act.wait_ge(pair_added, pair + 1)
                        nc.scalar.mul(picked[:, m, :, :, :].rearrange("p a c d -> p (a c d)"),
                                      ps_o[:, m, 0:2 * PARTS * HD], 1.0 / HEADS).then_inc(picked_ready, 1)

        @block.vector
        def _(v):
            v.sem_inc(scores_used, 2)
            steps = Steps(v, dve_step)
            gate = Gate(v, dve_passed)
            v.sem_inc(hits_ready, 1)
            v.wait_ge(be_loaded, 16)
            with v.Fori(0, TILES // UN) as it:
                for j in range(UN * HH):
                    u, h = j // HH, j % HH
                    s = it * (UN * HH) + j
                    if h == 0:
                        v.wait_ge(bias_ready, it * UN + (u + 1))
                    v.wait_ge(hits_ready, s + 1)
                    for c in range(CHUNKS):
                        gate.wait_ge(scores_ready, s * CHUNKS + (c + 1))
                        at = slice(c * SC, (c + 1) * SC)
                        nc.vector.tensor_tensor_reduce(
                            scores[:, at], ps_s[:, c % 2, :], bias[:, u, at], 1.0,
                            FLOOR if c == 0 else top[:, c - 1:c], ALU.add, ALU.max, top[:, c:c + 1])\
                            .then_inc(scores_used, 1)
                        v.wait_ge(scores_used, s * CHUNKS + (c + 3))
                    steps.turn(s)
                    steps.done(nc.vector.tensor_scalar(least[:], top[:, CHUNKS - 1:CHUNKS], be_col[:, 0:1],
                                                       TIE, ALU.add, ALU.subtract))
                    v.wait_ge(hits_turned, s * CHUNKS + CHUNKS)
                    nc.vector.tensor_scalar(hits[:, j % 2, :], scores[:], be_col[:, 0:1], least[:, 0:1],
                                            ALU.add, ALU.is_ge).then_inc(hits_ready, 1)


def layer1(nc, sem, adj_signs, x1_scr, u_scr, W_self, b_self, W_nb, b_nb, W_comb, b_comb, out):
    x1_v = x1_scr.rearrange("(b j e) f -> b e j f", j=P, e=2)
    x1_g = x1_scr.rearrange("(g b j e) f -> g j b (e f)", b=2, j=P, e=2)
    out_v = out.rearrange("(b j e) f -> b e j f", j=P, e=2)
    sign_v = adj_signs.rearrange("t p k -> (t p) k").rearrange("(b j e) k -> b e j k", j=P, e=2)
    with ExitStack() as outer:
        g_sb = outer.enter_context(nc.sbuf_tensor("g_parts", [P, TILES, PARTS, D], BF16))
        ident = outer.enter_context(nc.sbuf_tensor("l_ident", [P, P], F32))
        linear_maps(nc, sem, x1_g, u_scr, g_sb, ident, W_self, b_self, W_nb, b_nb, W_comb, b_comb)
        aggregation(nc, sem, x1_v, sign_v, u_scr, g_sb, ident, out_v)


def linear_maps(nc, sem, x1_g, u_scr, g_sb, ident, W_self, b_self, W_nb, b_nb, W_comb, b_comb):
    UN = 2
    OUTS = 2 * GT
    u_v = u_scr.rearrange("(g t) p f -> g t p f", t=GT)
    with ExitStack() as ctx:
        def sb(name, shape, dt):
            return ctx.enter_context(nc.sbuf_tensor(name, shape, dt))

        w_rows = sb("l_w_rows", [P, KC, D], F32)
        w_rowsT = sb("l_w_rowsT", [P, KC, D], F32)
        w_comb = sb("l_w_comb", [P, KC, D], F32)
        w = sb("l_w", [P, 2, KC, D], F32)
        b_cols = sb("l_b_cols", [P, 2 * KC], F32)
        b_wide = sb("l_b_wide", [P, 2 * KC, P], F32)
        b_row = sb("l_b_row", [P, D], F32)
        ones = sb("l_ones", [P, P], F32)
        xb = sb("l_x", [P, UN, GT, D], F32)
        xn = sb("l_xn", [P, GT, D], F32)
        hT = sb("l_hT", [P, UN, KC, GR], F32)
        stats = sb("l_stats", [P, GT, 6], F32)
        mv = sb("l_mv", [P, GT, 2], F32)
        small = sb("l_small", [P, 4, GT], F32)
        u_sb = sb("l_u", [P, 2, D], F32)
        value = sb("l_value", [P, 2, D], F32)
        rest = sb("l_rest", [P, D], F32)
        ps_t = ctx.enter_context(nc.psum_tensor("l_ps_t", [P, 2, D], F32))
        ps_o = ctx.enter_context(nc.psum_tensor("l_ps_o", [P, 4, D], F32))
        ps_b = ctx.enter_context(nc.psum_tensor("l_ps_b", [P, D], F32))

        ident_ready = sem("l_ident_ready")
        w_loaded = [sem(f"l_w_loaded{i}") for i in range(2)]
        b_loaded = sem("l_b_loaded")
        x_loaded = [sem(f"l_x_loaded{u}") for u in range(UN)]
        wide_ready = sem("l_wide_ready")
        bias_ready = sem("l_bias_ready")
        bias_kept = sem("l_bias_kept")
        var_ready = sem("l_var_ready")
        root_ready = sem("l_root_ready")
        xn_ready = sem("l_xn_ready")
        rows_turned = sem("l_rows_turned")
        turned_kept = sem("l_turned_kept")
        w_ready = sem("l_w_ready")
        w_kept = sem("l_w_kept")
        out_ready = sem("l_out_ready")
        value_ready = sem("l_value_ready")
        u_ready = sem("l_u_ready")
        value_split = sem("l_value_split")
        dve_step = sem("l_dve_step")
        u_stored = [sem(f"l_u_stored{a}") for a in range(2)]
        sp_passed = sem("l_sp_passed")
        dve_passed = sem("l_dve_passed")
        block = ctx.enter_context(nc.Block())

        W_FILLS = 2 * KC

        @block.gpsimd
        def _(pool):
            make_identity(nc, pool, ident, ident_ready)

        @block.sync
        def _(sp):
            sp_gate = Gate(sp, sp_passed)
            for i, b in enumerate((b_self, b_nb)):
                sp.dma_start(b_cols[:, i * KC:(i + 1) * KC], b.rearrange("(c p) -> p c", p=P),
                             allow_slow_non_contiguous=True).then_inc(b_loaded, 16)
            sp.dma_start(b_row[:], b_comb.rearrange("(a f) -> a f", a=1).broadcast_to([P, D])).then_inc(b_loaded, 16)
            sp.dma_start(w_rows[:], W_self.rearrange("(c p) f -> p c f", p=P)).then_inc(w_loaded[0], 16)
            sp.dma_start(w_comb[:], W_comb[0:D, :].rearrange("(c p) f -> p c f", p=P)).then_inc(w_loaded[0], 16)
            for u in range(UN):
                sp.dma_start(xb[:, u, :, :].rearrange("j (b e) f -> j b (e f)", e=2), x1_g[u, :, :, :])\
                  .then_inc(x_loaded[u], 16)
            sp_gate.wait_ge(w_ready, KC)
            sp.dma_start(w_rows[:], W_nb.rearrange("(c p) f -> p c f", p=P)).then_inc(w_loaded[1], 16)
            sp.dma_start(w_comb[:], W_comb[D:2 * D, :].rearrange("(c p) f -> p c f", p=P)).then_inc(w_loaded[1], 16)

            def group(g, u, last):
                if not last:
                    sp_gate.wait_ge(xn_ready, g + 1)
                    sp.dma_start(xb[:, u, :, :].rearrange("j (b e) f -> j b (e f)", e=2), x1_g[g + 2, :, :, :])\
                      .then_inc(x_loaded[u], 16)
                for t in range(GT):
                    sp_gate.wait_ge(u_ready, g * GT + (t + 1))
                    sp.dma_start(u_v[g, t, :, :], u_sb[:, t % 2, :]).then_inc(u_stored[t % 2], 16)

            with sp.Fori(0, GROUPS // UN - 1) as it:
                for u in range(UN):
                    group(it * UN + u, u, False)
            for u in range(UN):
                group(GROUPS - UN + u, u, True)
            for a in range(2):
                sp_gate.wait_ge(u_stored[a], TILES // 2 * 16)

        @block.tensor
        def _(pe):
            pe.wait_ge(ident_ready, 2)

            def turn_rows(g):
                pe.wait_ge(xn_ready, g + 1)
                for k in range(KC):
                    pe.wait_ge(turned_kept, g * KC + (W_FILLS + k + 1))
                    for t in range(GT):
                        last = nc.tensor.transpose(ps_t[:, k % 2, t * P:(t + 1) * P],
                                                   xn[:, t, k * P:(k + 1) * P], ident[:])
                    last.then_inc(rows_turned, 1)

            for i in range(2):
                pe.wait_ge(w_loaded[i], 32)
                for k in range(KC):
                    f = i * KC + k
                    pe.wait_ge(turned_kept, f + 1)
                    for c in range(KC):
                        last = nc.tensor.transpose(ps_t[:, f % 2, c * P:(c + 1) * P],
                                                   w_rows[:, c, k * P:(k + 1) * P], ident[:])
                    last.then_inc(rows_turned, 1)
                if i == 0:
                    pe.wait_ge(wide_ready, 2 * KC)
                for k in range(KC):
                    last = nc.tensor.matmul(ps_b[:], b_wide[:, i * KC + k, :], w_comb[:, k, :],
                                            start=i == 0 and k == 0, stop=i == 1 and k == KC - 1,
                                            skip_group_check=True)
                if i == 1:
                    last.then_inc(bias_ready, 1)
                pe.wait_ge(turned_kept, i * KC + KC + 2)
                for c in range(KC):
                    if i == 1:
                        pe.wait_ge(w_kept, c + 1)
                    for k in range(KC):
                        last = nc.tensor.matmul(ps_o[:, c, :], w_rowsT[:, k, c * P:(c + 1) * P], w_comb[:, k, :],
                                                start=k == 0, stop=k == KC - 1)
                    last.then_inc(w_ready, 1)

            def group(g, u, last_group):
                pe.wait_ge(turned_kept, g * KC + (W_FILLS + KC + 2))
                for o in range(OUTS):
                    t, i = o // 2, o % 2
                    if t < 2:
                        if not isinstance(g, int) or g > 0:
                            pe.wait_ge((u_ready, value_ready)[i], g * GT + (t - 1))
                    else:
                        pe.wait_ge((u_ready, value_ready)[i], g * GT + (t - 1))
                    for k in range(KC):
                        last = nc.tensor.matmul(ps_o[:, o % 4, :], hT[:, u, k, t * P:(t + 1) * P], w[:, i, k, :],
                                                start=k == 0, stop=k == KC - 1)
                    last.then_inc(out_ready, 1)
                    if o == 5 and not last_group:
                        turn_rows(g + 1)

            turn_rows(0)
            pe.wait_ge(w_kept, 2 * KC)
            group(0, 0, False)
            group(1, 1, False)
            with pe.Fori(1, GROUPS // UN - 1) as it:
                for u in range(UN):
                    group(it * UN + u, u, False)
            for u in range(UN):
                group(GROUPS - UN + u, u, u == UN - 1)

        @block.scalar
        def _(act):
            act.sem_inc(turned_kept, 2)
            for i in range(2):
                if i == 1:
                    act.wait_ge(w_ready, KC)
                for k in range(KC):
                    f = i * KC + k
                    act.wait_ge(rows_turned, f + 1)
                    nc.scalar.copy(w_rowsT[:, k, :], ps_t[:, f % 2, :]).then_inc(turned_kept, 1)
                for c in range(KC):
                    act.wait_ge(w_ready, i * KC + c + 1)
                    nc.scalar.copy(w[:, i, c, :], ps_o[:, c, :]).then_inc(w_kept, 1)

            def root(g):
                act.wait_ge(var_ready, g + 1)
                nc.scalar.activation(small[:, 1, :], small[:, 0, :], ACT.Sqrt).then_inc(root_ready, 1)

            def keep_rows(g, u):
                for k in range(KC):
                    act.wait_ge(rows_turned, g * KC + (W_FILLS + k + 1))
                    nc.scalar.activation(hT[:, u, k, :], ps_t[:, k % 2, :], ACT.Relu).then_inc(turned_kept, 1)

            def group(g, u, last_group):
                for t in range(GT):
                    if t == 2 and not last_group:
                        root(g + 1)
                    act.wait_ge(out_ready, g * OUTS + (2 * t + 2))
                    if t >= 2 or not isinstance(g, int) or g > 0:
                        act.wait_ge(value_split, g * GT + (t - 1))
                    nc.scalar.copy(value[:, t % 2, :], ps_o[:, 2 * (t % 2) + 1, :]).then_inc(value_ready, 1)
                    if t == 2 and not last_group:
                        keep_rows(g + 1, 1 - u)

            root(0)
            keep_rows(0, 0)
            group(0, 0, False)
            group(1, 1, False)
            with act.Fori(1, GROUPS // UN - 1) as it:
                for u in range(UN):
                    group(it * UN + u, u, False)
            for u in range(UN):
                group(GROUPS - UN + u, u, u == UN - 1)

        @block.vector
        def _(v):
            steps = Steps(v, dve_step)
            steps.done(nc.vector.memset(ones[:], 1.0))
            v.wait_ge(b_loaded, 3 * 16)
            for c in range(2 * KC):
                nc.vector.tensor_scalar(b_wide[:, c, :], ones[:], b_cols[:, c:c + 1], None, ALU.mult)\
                  .then_inc(wide_ready, 1)
            NORM = NORM_STEPS - 2
            PER = GT * SPLIT_STEPS + NORM

            def norm(g, u, it):
                v.wait_ge(x_loaded[u], it * 16 + 16)
                if not isinstance(g, int) or g > 0:
                    v.wait_ge(turned_kept, g * KC + (W_FILLS + 2))
                normalise(nc, v, Gate(v, dve_passed), steps, xb[:, u], xn, stats, mv, small, var_ready, root_ready, g)\
                    .then_inc(xn_ready, 1)

            def group(g, u, it, last_group):
                steps.turn(g * PER + (NORM + 1))
                for t in range(GT):
                    v.wait_ge(out_ready, g * OUTS + (2 * t + 1))
                    if not isinstance(g, int) or g * GT + t >= 2:
                        v.wait_ge(u_stored[t % 2], (g * 2 + t // 2) * 16)
                    nc.vector.tensor_tensor(u_sb[:, t % 2, :], ps_o[:, 2 * (t % 2), :], b_row[:], ALU.add)\
                      .then_inc(u_ready, 1)
                    v.wait_ge(value_ready, g * GT + (t + 1))
                    parts = [g_sb[:, bass.ds(g * GT + t, 1), n, :].rearrange("p a f -> p (a f)") for n in range(PARTS)]
                    split(nc, steps, value[:, t % 2, :], rest[:], *parts).then_inc(value_split, 1)
                    if t == 1 and not last_group:
                        norm(g + 1, 1 - u, it + u)

            norm(0, 0, 0)
            v.wait_ge(bias_ready, 1)
            nc.vector.tensor_tensor(b_row[:], ps_b[:], b_row[:], ALU.add).then_inc(bias_kept, 1)
            v.wait_ge(bias_kept, 1)
            group(0, 0, 0, False)
            group(1, 1, 0, False)
            with v.Fori(1, GROUPS // UN - 1) as it:
                for u in range(UN):
                    group(it * UN + u, u, it, False)
            for u in range(UN):
                group(GROUPS - UN + u, u, GROUPS // UN - 1, u == UN - 1)


def aggregation(nc, sem, x1_v, sign_v, u_scr, g_sb, ident, out_v):
    UN = 2
    with ExitStack() as ctx:
        def sb(name, shape, dt):
            return ctx.enter_context(nc.sbuf_tensor(name, shape, dt))

        signs = sb("g_signs", [P, UN, N], I8)
        mask = sb("g_mask", [P, UN, N], BF16)
        maskT = sb("g_maskT", [P, UN, BLOCKS, P, 2], BF16)
        deg = sb("g_deg", [P, UN, 3], F32)
        u_sb = sb("g_u", [P, UN, D], F32)
        x1 = sb("g_x1", [P, UN, D], F32)
        mixed = sb("g_mixed", [P, D], F32)
        y = sb("g_y", [P, UN, D], F32)
        ps_t = ctx.enter_context(nc.psum_tensor("g_ps_t", [P, 2, TB * P], F32))
        ps_o = ctx.enter_context(nc.psum_tensor("g_ps_o", [P, 2, D], F32))

        signs_loaded = [sem(f"g_signs_loaded{u}") for u in range(UN)]
        rows_loaded = [sem(f"g_rows_loaded{u}") for u in range(UN)]
        mask_ready = sem("g_mask_ready")
        deg_ready = sem("g_deg_ready")
        mask_turned = sem("g_mask_turned")
        turned_kept = sem("g_turned_kept")
        sum_ready = sem("g_sum_ready")
        sum_used = sem("g_sum_used")
        y_ready = sem("g_y_ready")
        y_stored = [sem(f"g_y_stored{u}") for u in range(UN)]
        sp_passed = sem("g_sp_passed")
        block = ctx.enter_context(nc.Block())

        @block.sync
        def _(sp):
            sp_gate = Gate(sp, sp_passed)
            def load_signs(b, u):
                sp.dma_start(signs[:, u, :], sign_v[b, u, :, :]).then_inc(signs_loaded[u], 16)

            def load_rows(b, u):
                sp.dma_start(u_sb[:, u, :], u_scr[b * 2 + u, :, :]).then_inc(rows_loaded[u], 16)
                sp.dma_start(x1[:, u, :], x1_v[b, u, :, :]).then_inc(rows_loaded[u], 16)

            def store(b, u):
                sp_gate.wait_ge(y_ready, b * 2 + (u + 1))
                sp.dma_start(out_v[b, u, :, :], y[:, u, :]).then_inc(y_stored[u], 16)

            for u in range(UN):
                load_signs(0, u)
            for u in range(UN):
                load_rows(0, u)
            with sp.Fori(1, BLOCKS) as b:
                for u in range(UN):
                    sp_gate.wait_ge(mask_ready, b * 2 + (u - 1))
                    load_signs(b, u)
                    store(b - 1, u)
                    load_rows(b, u)
            for u in range(UN):
                store(BLOCKS - 1, u)
            for u in range(UN):
                sp_gate.wait_ge(y_stored[u], BLOCKS * 16)

        @block.tensor
        def _(pe):
            def turn_chunk(n, u, c):
                if c == 0:
                    pe.wait_ge(mask_ready, n + 1)
                pe.wait_ge(turned_kept, n * CHUNKS + (c + 1))
                pairs = mask[:, u, :].bitcast(F32)
                for b in range(TB):
                    at = (c * TB + b) * P
                    last = nc.tensor.transpose(ps_t[:, c % 2, b * P:(b + 1) * P], pairs[:, at:at + P], ident[:])
                last.then_inc(mask_turned, 1)

            def sum_chunk(n, u, c):
                pe.wait_ge(turned_kept, n * CHUNKS + (c + 3))
                if c == 0:
                    pe.wait_ge(sum_used, n + 1)
                for b in range(c * TB, (c + 1) * TB):
                    for e in range(2):
                        for part in range(PARTS):
                            last = nc.tensor.matmul(ps_o[:, u, :], maskT[:, u, b, :, e], g_sb[:, 2 * b + e, part, :],
                                                    start=b == 0 and e == 0 and part == 0,
                                                    stop=b == BLOCKS - 1 and e == 1 and part == PARTS - 1)
                if c == CHUNKS - 1:
                    last.then_inc(sum_ready, 1)

            def tile(n, u, last):
                for c in range(CHUNKS):
                    sum_chunk(n, u, c)
                    if not last:
                        turn_chunk(n + 1, 1 - u, c)

            for c in range(CHUNKS):
                turn_chunk(0, 0, c)
            with pe.Fori(0, BLOCKS - 1) as b:
                for u in range(UN):
                    tile(b * 2 + u, u, False)
            for u in range(UN):
                tile(TILES - UN + u, u, u == UN - 1)

        @block.scalar
        def _(act):
            act.sem_inc(turned_kept, 2)

            def keep(n, u, b):
                if not isinstance(b, int) or b > 0:
                    act.wait_ge(sum_ready, n - 1)
                for c in range(CHUNKS):
                    act.wait_ge(mask_turned, n * CHUNKS + (c + 1))
                    nc.scalar.copy(maskT[:, u, c * TB:(c + 1) * TB, :, :].rearrange("p b q e -> p (b q e)"),
                                   ps_t[:, c % 2, :].bitcast(BF16)).then_inc(turned_kept, 1)

            for u in range(UN):
                keep(u, u, 0)
            with act.Fori(1, BLOCKS) as b:
                for u in range(UN):
                    keep(b * 2 + u, u, b)

        @block.vector
        def _(v):
            v.sem_inc(sum_used, 2)

            def masks(n, u, b):
                v.wait_ge(signs_loaded[u], b * 16 + 16)
                if not isinstance(n, int) or n >= 2:
                    v.wait_ge(mask_turned, (n - 1) * CHUNKS)
                nc.vector.tensor_scalar(mask[:, u, :], signs[:, u, :], 0.0, 0.0, ALU.is_gt, ALU.add,
                                        accum_out=deg[:, u, 0:1]).then_inc(mask_ready, 1)
                v.wait_ge(mask_ready, n + 1)
                nc.vector.tensor_scalar(deg[:, u, 1:2], deg[:, u, 0:1], 1.0, None, ALU.max).then_inc(deg_ready, 1)
                v.wait_ge(deg_ready, n * 2 + 1)
                nc.vector.reciprocal(deg[:, u, 2:3], deg[:, u, 1:2]).then_inc(deg_ready, 1)

            def finish(n, u, b):
                if not isinstance(n, int) or n > 0:
                    v.wait_ge(y_ready, n)
                v.wait_ge(sum_ready, n + 1)
                v.wait_ge(rows_loaded[u], b * 32 + 32)
                v.wait_ge(deg_ready, n * 2 + 2)
                nc.vector.scalar_tensor_tensor(mixed[:], ps_o[:, u, :], deg[:, u, 2:3], u_sb[:, u, :],
                                               ALU.mult, ALU.add).then_inc(sum_used, 1)
                v.wait_ge(sum_used, n + 3)
                if not isinstance(b, int) or b > 0:
                    v.wait_ge(y_stored[u], b * 16)
                nc.vector.scalar_tensor_tensor(y[:, u, :], mixed[:], 0.0, x1[:, u, :],
                                               ALU.max, ALU.add).then_inc(y_ready, 1)

            masks(0, 0, 0)
            masks(1, 1, 0)
            finish(0, 0, 0)
            with v.Fori(1, BLOCKS) as b:
                masks(b * 2, 0, b)
                finish(b * 2 - 1, 1, b - 1)
                masks(b * 2 + 1, 1, b)
                finish(b * 2, 0, b)
            finish(TILES - 1, 1, BLOCKS - 1)


def two_layers(nc, x, adj, WQ, WK, WV, we, be, W_self, b_self, W_nb, b_nb, W_comb, b_comb, out):
    def scratch(name, shape, dt):
        return nc.dram_tensor(name, shape, dt).ap()

    q_scr = scratch("q_scr", [HEADS, 3, P, N], BF16)
    k_scr = scratch("k_scr", [HEADS, 2, P, N], BF16)
    v_scr = scratch("v_scr", [N, PARTS, D], BF16)
    sign_scr = scratch("sign_scr", [TILES, P, N], I8)
    x1_scr = scratch("x1_scr", [N, D], F32)
    u_scr = scratch("u_scr", [TILES, P, D], F32)
    with ExitStack() as sems:
        def sem(name):
            return sems.enter_context(nc.semaphore(name))

        projections(nc, sem, x, adj, WQ, WK, WV, we, q_scr, k_scr, v_scr, sign_scr)
        for half in range(HEADS // HH):
            attention(nc, sem, half, x, be, q_scr, k_scr, v_scr, sign_scr, x1_scr)
        layer1(nc, sem, sign_scr, x1_scr, u_scr, W_self, b_self, W_nb, b_nb, W_comb, b_comb, out)


_INS = ["x", "adj", "L0_gnn_WQ", "L0_gnn_WK", "L0_gnn_WV", "L0_gnn_we", "L0_gnn_be",
        "L1_gnn_W_self", "L1_gnn_b_self", "L1_gnn_W_nb", "L1_gnn_b_nb", "L1_gnn_W_comb", "L1_gnn_b_comb"]


def kernel(**inputs):
    import numpy as _np
    import concourse.bacc as _bacc
    from concourse import mybir as _mybir
    from concourse.bass_utils import run_bass_kernel_spmd as _run

    nc = _bacc.Bacc("TRN2", target_bir_lowering=False, num_devices=1)
    arrays, args = {}, []
    for name in _INS:
        a = _np.ascontiguousarray(inputs[name])
        arrays[f"in_{name}_dram"] = a
        args.append(nc.dram_tensor(f"in_{name}_dram", a.shape, _mybir.dt.from_np(a.dtype), kind="ExternalInput").ap())
    args.append(nc.dram_tensor("out_0_dram", (N, D), F32, kind="ExternalOutput").ap())
    two_layers(nc, *args)
    r = _run(nc, [arrays], core_ids=[0])
    return r.results[0]["out_0_dram"]
```

```python
from contextlib import ExitStack

import concourse.bass as bass
from concourse import mybir

F32 = mybir.dt.float32
BF16 = mybir.dt.bfloat16
F32R = mybir.dt.float32r
I8 = mybir.dt.int8
U16 = mybir.dt.uint16
F8 = mybir.dt.float8e4
I32 = mybir.dt.int32
ALU = mybir.AluOpType
ACT = mybir.ActivationFunctionType

P = 128
N = 4096
D = 512
HEADS = 8
HD = D // HEADS
KC = D // P
TILES = N // P
GT = 4
GROUPS = TILES // GT
GR = GT * P
PARTS = 3
RPARTS = 2
E = 4
BLOCKS = N // (E * P)
EPS = 1e-5
SCALING = HD ** -0.5
HH = 4
HALF = HH * HD
SC = 1024
CHUNKS = N // SC
TB = BLOCKS // CHUNKS
MASKED = -1e30
FLOOR = -1e29
TIE = 2.0 ** -25


class Steps:

    def __init__(self, engine, sem):
        self.engine, self.sem, self.base, self.n = engine, sem, 0, 0

    def turn(self, base):
        self.base, self.n = base, 0

    def done(self, instruction):
        self.n += 1
        instruction.then_inc(self.sem, 1)
        self.engine.wait_ge(self.sem, self.base + self.n)


class Gate:

    def __init__(self, engine, sem):
        self.engine, self.sem = engine, sem

    def wait_ge(self, sem, value):
        self.engine.wait_ge(sem, value)
        self.engine.sem_inc(self.sem, 1)


def make_identity(nc, pool, ident, sem):
    nc.gpsimd.memset(ident[:], 0.0).then_inc(sem, 1)
    pool.wait_ge(sem, 1)
    nc.gpsimd.affine_select(out=ident[:], in_=ident[:], compare_op=ALU.not_equal, fill=1.0, base=0,
                            pattern=[[-1, P]], channel_multiplier=1).then_inc(sem, 1)


NORM_STEPS = 2 * GT + 7


def normalise(nc, v, gate, steps, x, xn, stats, mv, small, var_ready, root_ready, turn):
    for t in range(GT):
        nc.vector.bn_stats(stats[:, t, :], x[:, t, :]).then_inc(steps.sem, 1)
        steps.n += 1
    gate.wait_ge(steps.sem, steps.base + steps.n)
    for t in range(GT):
        nc.vector.bn_aggr(mv[:, t, :], stats[:, t, :]).then_inc(steps.sem, 1)
        steps.n += 1
    v.wait_ge(steps.sem, steps.base + steps.n)
    var, root, inv, other = (small[:, i, :] for i in range(4))
    nc.vector.tensor_scalar(var, mv[:, :, 1], EPS, None, ALU.add).then_inc(var_ready, 1)
    v.wait_ge(root_ready, turn + 1)
    steps.done(nc.vector.reciprocal(inv, root))
    steps.done(nc.vector.tensor_tensor(other, var, inv, ALU.mult))
    steps.done(nc.vector.tensor_tensor(other, other, root, ALU.add))
    steps.done(nc.vector.tensor_scalar(other, other, 0.5, None, ALU.mult))
    steps.done(nc.vector.reciprocal(inv, other))
    for t in range(GT):
        last = nc.vector.tensor_scalar(xn[:, t, :], x[:, t, :], mv[:, t, 0:1], inv[:, t:t + 1],
                                       ALU.subtract, ALU.mult)
    return last


SPLIT_STEPS = 3
SPLIT_R_STEPS = 1


def split_r(nc, steps, value, high, low):
    steps.done(nc.vector.tensor_copy(high, value))
    return nc.vector.tensor_tensor(low, value, high.bitcast(F32), ALU.subtract)


def split(nc, steps, value, rest, high, middle, low):
    steps.done(nc.vector.tensor_copy(high, value))
    steps.done(nc.vector.tensor_tensor(rest, value, high, ALU.subtract))
    steps.done(nc.vector.tensor_copy(middle, rest))
    return nc.vector.tensor_tensor(low, rest, middle, ALU.subtract)


def projections(nc, sem, x, WQ, WK, WV, we, q_scr, k_scr, v_scr):
    x_v = x.rearrange("(g t p) f -> g p t f", t=GT, p=P)
    v_v = v_scr.rearrange("h (g t p) c f -> g t p h (c f)", t=GT, p=P)
    UN = 2
    OUTS = 3 * KC
    STORES = 2 * RPARTS
    NEXT_AT = 8

    with ExitStack() as ctx:
        def sb(name, shape, dt):
            return ctx.enter_context(nc.sbuf_tensor(name, shape, dt))

        ident = sb("p_ident", [P, P], F32)
        w_rows = sb("p_w_rows", [P, 3, KC, D], F32)
        wT = sb("p_wT", [P, 3, KC, D], F32)
        we_col = sb("p_we_col", [P, 1], F32)
        xb = sb("p_x", [P, UN, GT, D], F32)
        xn = sb("p_xn", [P, GT, D], F32)
        hT = sb("p_hT", [P, UN, KC, GR], F32)
        stats = sb("p_stats", [P, GT, 6], F32)
        mv = sb("p_mv", [P, GT, 2], F32)
        small = sb("p_small", [P, 4, GT], F32)
        value = sb("p_value", [P, 2, D], F32)
        rest = sb("p_rest", [P, D], F32)
        k_parts = sb("p_k_parts", [P, RPARTS, KC, GR], F32R)
        q_parts = sb("p_q_parts", [P, RPARTS, KC, GR], F32R)
        v_parts = sb("p_v_parts", [P, GT, HEADS, PARTS, HD], BF16)
        ps_t = ctx.enter_context(nc.psum_tensor("p_ps_t", [P, 2, D], F32))
        ps_o = ctx.enter_context(nc.psum_tensor("p_ps_o", [P, 4, D], F32))

        w_loaded = [sem(f"p_w_loaded{i}") for i in range(3)]
        we_loaded = sem("p_we_loaded")
        ident_ready = sem("p_ident_ready")
        x_loaded = [sem(f"p_x_loaded{u}") for u in range(UN)]
        var_ready = sem("p_var_ready")
        root_ready = sem("p_root_ready")
        xn_ready = sem("p_xn_ready")
        rows_turned = sem("p_rows_turned")
        turned_kept = sem("p_turned_kept")
        out_ready = sem("p_out_ready")
        value_ready = sem("p_value_ready")
        value_split = sem("p_value_split")
        dve_step = sem("p_dve_step")
        k_stored = sem("p_k_stored")
        q_stored = sem("p_q_stored")
        v_stored = sem("p_v_stored")
        sp_passed = sem("p_sp_passed")
        dve_passed = sem("p_dve_passed")
        block = ctx.enter_context(nc.Block())

        W_FILLS = 3 * KC

        @block.gpsimd
        def _(pool):
            make_identity(nc, pool, ident, ident_ready)

        @block.sync
        def _(sp):
            sp_gate = Gate(sp, sp_passed)
            for i, w in enumerate((WK, WQ, WV)):
                sp.dma_start(w_rows[:, i, :, :], w.rearrange("(c p) f -> p c f", p=P)).then_inc(w_loaded[i], 16)
                if i < UN:
                    sp.dma_start(xb[:, i, :, :], x_v[i, :, :, :]).then_inc(x_loaded[i], 16)
            for a in range(2):
                sp.dma_start(we_col[a * HD:(a + 1) * HD, :], we.rearrange("a d -> d a")).then_inc(we_loaded, 16)

            def group(g, u, last_x):
                for t in range(1, GT):
                    if t == 1:
                        sp_gate.wait_ge(value_split, g * OUTS + (2 + KC))
                        for part in range(RPARTS):
                            for a in range(2):
                                sp.dma_start(
                                    k_scr[a::2, part * HD:(part + 1) * HD, bass.ts(g, GR)].rearrange("c p r -> p c r"),
                                    k_parts[a * HD:(a + 1) * HD, part, :, :].bitcast(F32)).then_inc(k_stored, 16)
                    if t == 2:
                        sp_gate.wait_ge(value_split, g * OUTS + (2 + 2 * KC))
                        for part in range(RPARTS):
                            for a in range(2):
                                sp.dma_start(
                                    q_scr[a::2, part, :, bass.ts(g, GR)].rearrange("c p r -> p c r"),
                                    q_parts[a * HD:(a + 1) * HD, part, :, :].bitcast(F32)).then_inc(q_stored, 16)
                    if t == 3:
                        if not last_x:
                            sp_gate.wait_ge(xn_ready, g + 1)
                            sp.dma_start(xb[:, u, :, :], x_v[g + 2, :, :, :]).then_inc(x_loaded[u], 16)
                        sp_gate.wait_ge(value_split, g * OUTS + (2 + 3 * KC))
                        for i in range(GT):
                            sp.dma_start(v_v[g, i, :, :, :], v_parts[:, i, :, :, :].rearrange("p h c d -> p h (c d)"))\
                              .then_inc(v_stored, 16)

            with sp.Fori(0, GROUPS // UN - 1) as it:
                for u in range(UN):
                    group(it * UN + u, u, False)
            for u in range(UN):
                group(GROUPS - UN + u, u, True)
            sp_gate.wait_ge(k_stored, GROUPS * STORES * 16)
            sp_gate.wait_ge(q_stored, GROUPS * STORES * 16)
            sp_gate.wait_ge(v_stored, GROUPS * GT * 16)

        @block.tensor
        def _(pe):
            pe.wait_ge(ident_ready, 2)
            for f in range(W_FILLS):
                i, k = f // KC, f % KC
                if k == 0:
                    pe.wait_ge(w_loaded[i], 16)
                pe.wait_ge(turned_kept, f + 1)
                for c in range(KC):
                    last = nc.tensor.transpose(ps_t[:, f % 2, c * P:(c + 1) * P],
                                               w_rows[:, i, c, k * P:(k + 1) * P], ident[:])
                last.then_inc(rows_turned, 1)

            def turn_rows(g):
                pe.wait_ge(xn_ready, g + 1)
                for k in range(KC):
                    pe.wait_ge(turned_kept, g * KC + (W_FILLS + k + 1))
                    for t in range(GT):
                        last = nc.tensor.transpose(ps_t[:, k % 2, t * P:(t + 1) * P],
                                                   xn[:, t, k * P:(k + 1) * P], ident[:])
                    last.then_inc(rows_turned, 1)

            def group(g, u, last_group):
                pe.wait_ge(turned_kept, g * KC + (W_FILLS + KC + 2))
                for o in range(OUTS):
                    pe.wait_ge(value_ready, g * OUTS + (o + 1))
                    i, c = o // KC, o % KC
                    for k in range(KC):
                        if i < 2:
                            lhsT, rhs = wT[:, i, k, c * P:(c + 1) * P], hT[:, u, k, :]
                        else:
                            lhsT, rhs = hT[:, u, k, c * P:(c + 1) * P], wT[:, i, k, :]
                        last = nc.tensor.matmul(ps_o[:, o % 4, :], lhsT, rhs, start=k == 0, stop=k == KC - 1)
                    last.then_inc(out_ready, 1)
                    if o == NEXT_AT and not last_group:
                        turn_rows(g + 1)

            turn_rows(0)
            with pe.Fori(0, GROUPS // UN - 1) as it:
                for u in range(UN):
                    group(it * UN + u, u, False)
            for u in range(UN):
                group(GROUPS - UN + u, u, u == UN - 1)

        @block.scalar
        def _(act):
            act.sem_inc(turned_kept, 2)
            act.sem_inc(value_ready, 4)
            for f in range(W_FILLS):
                act.wait_ge(rows_turned, f + 1)
                nc.scalar.copy(wT[:, f // KC, f % KC, :], ps_t[:, f % 2, :]).then_inc(turned_kept, 1)
            act.wait_ge(we_loaded, 32)

            def root(g):
                act.wait_ge(var_ready, g + 1)
                nc.scalar.activation(small[:, 1, :], small[:, 0, :], ACT.Sqrt).then_inc(root_ready, 1)

            def keep_rows(g, u):
                for k in range(KC):
                    act.wait_ge(rows_turned, g * KC + (W_FILLS + k + 1))
                    nc.scalar.activation(hT[:, u, k, :], ps_t[:, k % 2, :], ACT.Relu).then_inc(turned_kept, 1)

            def group(g, u, last_group):
                for o in range(OUTS):
                    if o == 5 and not last_group:
                        root(g + 1)
                    act.wait_ge(out_ready, g * OUTS + (o + 1))
                    act.wait_ge(value_split, g * OUTS + (o + 1))
                    if o < KC:
                        nc.scalar.activation(value[:, o % 2, :], ps_o[:, o % 4, :], ACT.Identity,
                                             bias=we_col[:, 0:1], scale=SCALING).then_inc(value_ready, 1)
                    else:
                        nc.scalar.copy(value[:, o % 2, :], ps_o[:, o % 4, :]).then_inc(value_ready, 1)
                    if o == NEXT_AT and not last_group:
                        keep_rows(g + 1, 1 - u)

            root(0)
            keep_rows(0, 0)
            group(0, 0, False)
            group(1, 1, False)
            with act.Fori(1, GROUPS // UN - 1) as it:
                for u in range(UN):
                    group(it * UN + u, u, False)
            for u in range(UN):
                group(GROUPS - UN + u, u, u == UN - 1)

        @block.vector
        def _(v):
            v.sem_inc(value_split, 2)
            steps = Steps(v, dve_step)
            NORM = NORM_STEPS - 2
            PER = KC * (2 * SPLIT_R_STEPS + SPLIT_STEPS) + NORM

            def norm(g, u, it):
                v.wait_ge(x_loaded[u], it * 16 + 16)
                if not isinstance(g, int) or g > 0:
                    v.wait_ge(turned_kept, g * KC + (W_FILLS + 2))
                normalise(nc, v, Gate(v, dve_passed), steps, xb[:, u], xn, stats, mv, small, var_ready, root_ready, g)\
                    .then_inc(xn_ready, 1)

            def group(g, u, it, last_group):
                steps.turn(g * PER + NORM)
                for o in range(OUTS):
                    i, c = o // KC, o % KC
                    v.wait_ge(value_ready, g * OUTS + (o + 5))
                    if not isinstance(g, int) or g > 0:
                        if o == 0:
                            v.wait_ge(k_stored, g * (STORES * 16))
                        if o == KC:
                            v.wait_ge(q_stored, g * (STORES * 16))
                        if o == 2 * KC:
                            v.wait_ge(v_stored, g * (GT * 16))
                    whole = value[:, o % 2, :]
                    if i < 2:
                        to = (k_parts, q_parts)[i]
                        last = split_r(nc, steps, whole, *(to[:, n, c, :] for n in range(RPARTS)))
                    else:
                        whole, left = (a.rearrange("p (h d) -> p h d", d=HD) for a in (whole, rest[:]))
                        last = split(nc, steps, whole, left, *(v_parts[:, c, :, n, :] for n in range(PARTS)))
                    last.then_inc(value_split, 1)
                    if o == 3 and not last_group:
                        norm(g + 1, 1 - u, it + u)

            steps.turn(0)
            norm(0, 0, 0)
            assert steps.n == NORM, steps.n
            group(0, 0, 0, False)
            assert steps.n == PER, steps.n
            group(1, 1, 0, False)
            with v.Fori(1, GROUPS // UN - 1) as it:
                for u in range(UN):
                    group(it * UN + u, u, it, False)
            for u in range(UN):
                group(GROUPS - UN + u, u, GROUPS // UN - 1, u == UN - 1)


def attention(nc, sem, x, adj, be, q_scr, k_scr, v_scr, sign_scr, x1_scr):
    n_ = "a_"
    HALVES = HEADS // HH
    v_v = v_scr.rearrange("h (b j e) c d -> h j b (e c d)", j=P, e=E)
    adj_v = adj.rearrange("(t p) k -> t p k", p=P)
    x_v = x.rearrange("(t p) f -> t p f", p=P)
    x1_v = x1_scr.rearrange("(t p) f -> t p f", p=P)
    UN = 2
    LAG = 2
    TILE_CHUNKS = HH * CHUNKS
    PAIRS = HH // 2
    HN = N // 2
    TURNS = TILES // UN

    with ExitStack() as ctx:
        def sb(name, shape, dt):
            return ctx.enter_context(nc.sbuf_tensor(n_ + name, shape, dt))

        ident = sb("ident", [P, P], F32)
        be_col = sb("be", [P, 1], F32)
        k_sb = sb("k", [P, HH, N], F32R)
        v_sb = sb("v", [P, HH, BLOCKS, E, PARTS, HD], BF16)
        q_sb = sb("q", [P, UN, HH, RPARTS, P], F32R)
        adj_rows = sb("adj", [P, 2, HN], I32)
        signs = sb("signs", [P, UN, N], I8)
        bias = sb("bias", [P, UN, N], BF16)
        scores = sb("scores", [P, N], F32)
        top = sb("top", [P, CHUNKS], F32)
        least = sb("least", [P, 2], F32)
        hits = sb("hits", [P, 2, N], F8)
        hitsT = sb("hitsT", [P, CHUNKS, TB, P, E], F8)
        xt = sb("xt", [P, UN, HALF], F32)
        picked = sb("picked", [P, 2, 2, PARTS, HD], F32)
        ps_s = ctx.enter_context(nc.psum_tensor(n_ + "ps_s", [P, 2, SC], F32))
        ps_t = ctx.enter_context(nc.psum_tensor(n_ + "ps_t", [P, 2, 512], F32))
        ps_o = ctx.enter_context(nc.psum_tensor(n_ + "ps_o", [P, 2, 512], F32))

        ident_ready = sem(n_ + "ident_ready")
        be_loaded = sem(n_ + "be_loaded")
        k_loaded = [sem(n_ + f"k_loaded{h}") for h in range(HH)]
        v_loaded = [sem(n_ + f"v_loaded{h}") for h in range(HH)]
        q_loaded = [sem(n_ + f"q_loaded{u}") for u in range(UN)]
        adj_loaded = [sem(n_ + f"adj_loaded{i}") for i in range(2)]
        signs_ready = sem(n_ + "signs_ready")
        signs_stored = [sem(n_ + f"signs_stored{u}") for u in range(UN)]
        signs_loaded = [sem(n_ + f"signs_loaded{u}") for u in range(UN)]
        x_loaded = [sem(n_ + f"x_loaded{u}") for u in range(UN)]
        bias_ready = sem(n_ + "bias_ready")
        scores_ready = sem(n_ + "scores_ready")
        scores_used = sem(n_ + "scores_used")
        dve_step = sem(n_ + "dve_step")
        hits_ready = sem(n_ + "hits_ready")
        hits_turned = sem(n_ + "hits_turned")
        turned_kept = sem(n_ + "turned_kept")
        turned_used = sem(n_ + "turned_used")
        out_ready = sem(n_ + "out_ready")
        picked_ready = sem(n_ + "picked_ready")
        pool_step = sem(n_ + "pool_step")
        pair_added = sem(n_ + "pair_added")
        x1_stored = [sem(n_ + f"x1_stored{u}") for u in range(UN)]
        sp_passed = sem(n_ + "sp_passed")
        dve_passed = sem(n_ + "dve_passed")
        pe_passed = sem(n_ + "pe_passed")
        pool_passed = sem(n_ + "pool_passed")
        block = ctx.enter_context(nc.Block())

        @block.sync
        def _(sp):
            sp_gate = Gate(sp, sp_passed)
            sp.dma_start(be_col[:], be.rearrange("(a b) -> a b", a=1).broadcast_to([P, 1])).then_inc(be_loaded, 16)

            def load_k(half, h):
                sp.dma_start(k_sb[:, h, :].bitcast(F32), k_scr[half * HH + h, :, :])\
                  .then_inc(k_loaded[h], 16)

            def load_v(half, h):
                sp.dma_start(v_sb[:, h].rearrange("j b e c d -> j b (e c d)"), v_v[half * HH + h, :, :, :])\
                  .then_inc(v_loaded[h], 16)

            def load_q(half, t, u):
                for at in range(0, P, HD):
                    sp.dma_start(q_sb[at:at + HD, u, :, :, :].rearrange("p h s r -> p (h s) r").bitcast(F32),
                                 q_scr[half * HH:(half + 1) * HH, :, :, bass.ts(t, P)].rearrange("h s p r -> p (h s) r"))\
                      .then_inc(q_loaded[u], 16)

            def load_signs(t, u):
                sp.dma_start(signs[:, u, :], sign_scr[t, :, :]).then_inc(signs_loaded[u], 16)

            def load_adj(t):
                for i in range(2):
                    if not isinstance(t, int) or t > 0:
                        sp_gate.wait_ge(bias_ready, (t - 1) * 2 + (i + 1))
                        sp_gate.wait_ge(signs_ready, (t - 1) * 2 + (i + 1))
                    sp.dma_start(adj_rows[:, i, :], adj_v[t, :, i * HN:(i + 1) * HN]).then_inc(adj_loaded[i], 16)

            def store_signs(t, u):
                sp_gate.wait_ge(signs_ready, t * 2 + 2)
                sp.dma_start(sign_scr[t, :, :], signs[:, u, :]).then_inc(signs_stored[u], 16)

            def load_x(half, t, u):
                sp.dma_start(xt[:, u, :], x_v[t, :, half * HALF:(half + 1) * HALF]).then_inc(x_loaded[u], 16)

            def store(half, t, u):
                sp_gate.wait_ge(pair_added, (t + half * TILES) * PAIRS + (PAIRS + 2))
                sp.dma_start(x1_v[t, :, half * HALF:(half + 1) * HALF], xt[:, u, :]).then_inc(x1_stored[u], 16)

            def next_tile(half, t, u, stored_half, stored, turns):
                number = t + half * TILES
                if half == 0:
                    load_adj(t)
                    store_signs(t - 1, 1 - u)
                else:
                    sp_gate.wait_ge(bias_ready, (number - 1) * 2)
                    load_signs(t, u)
                sp_gate.wait_ge(scores_ready, (number - 1) * TILE_CHUNKS)
                load_q(half, t, u)
                store(stored_half, stored, u)
                sp_gate.wait_ge(x1_stored[u], turns * 16)
                load_x(half, t, u)

            load_adj(0)
            load_q(0, 0, 0)
            load_k(0, 0)
            load_k(0, 1)
            load_v(0, 0)
            load_adj(1)
            store_signs(0, 0)
            load_k(0, 2)
            load_q(0, 1, 1)
            load_v(0, 1)
            load_k(0, 3)
            load_x(0, 0, 0)
            load_v(0, 2)
            load_v(0, 3)
            load_x(0, 1, 1)
            for half in range(HALVES):
                if half:
                    if half == 1:
                        store_signs(TILES - 1, 1)
                        for u in range(UN):
                            sp_gate.wait_ge(signs_stored[u], TURNS * 16)
                    sp_gate.wait_ge(bias_ready, (half * TILES - 1) * 2)
                    load_signs(0, 0)
                    sp_gate.wait_ge(scores_ready, (half * TILES - 1) * TILE_CHUNKS)
                    load_q(half, 0, 0)
                    for h in range(HH):
                        step = half * TILES * HH - HH + h
                        sp_gate.wait_ge(scores_ready, (step + 1) * CHUNKS)
                        load_k(half, h)
                        if h >= LAG:
                            sp_gate.wait_ge(turned_used, (step + 1 - LAG) * CHUNKS + 4)
                            load_v(half, h - LAG)
                        if h == 0:
                            store(half - 1, TILES - UN, 0)
                            sp_gate.wait_ge(x1_stored[0], half * (TILES // UN) * 16)
                            load_x(half, 0, 0)
                            sp_gate.wait_ge(bias_ready, half * TILES * 2)
                            load_signs(1, 1)
                    sp_gate.wait_ge(scores_ready, half * TILES * TILE_CHUNKS)
                    load_q(half, 1, 1)
                    for h in range(HH - LAG, HH):
                        sp_gate.wait_ge(turned_used, (half * TILES * HH - HH + h + 1) * CHUNKS + 4)
                        load_v(half, h)
                    store(half - 1, TILES - 1, 1)
                    sp_gate.wait_ge(x1_stored[1], half * (TILES // UN) * 16)
                    load_x(half, 1, 1)
                with sp.Fori(1, TILES // UN) as it:
                    for u in range(UN):
                        t = it * UN + u
                        next_tile(half, t, u, half, t - 2, it + half * (TILES // UN))
            for u in range(UN):
                store(HALVES - 1, TILES - UN + u, u)
            for u in range(UN):
                sp_gate.wait_ge(x1_stored[u], HALVES * (TILES // UN) * 16)

        @block.gpsimd
        def _(pool):
            make_identity(nc, pool, ident, ident_ready)
            pool.sem_inc(pair_added, 2)
            steps = Steps(pool, pool_step)
            gate = Gate(pool, pool_passed)

            def make_bias(number, u, turn, half):
                for i in range(2):
                    if half == 0:
                        source = adj_rows[:, i, :]
                        pool.wait_ge(adj_loaded[i], number * 16 + 16)
                    else:
                        source = signs[:, u, i * HN:(i + 1) * HN]
                        pool.wait_ge(signs_loaded[u], (turn - TURNS) * 16 + 16)
                    if not isinstance(number, int):
                        gate.wait_ge(scores_used, (number - 1) * TILE_CHUNKS + 2)
                    nc.gpsimd.tensor_scalar(bias[:, u, i * HN:(i + 1) * HN], source, 0.0, MASKED, ALU.is_le, ALU.mult)\
                      .then_inc(bias_ready, 1)

            def add_pairs(number, u, turn):
                pool.wait_ge(x_loaded[u], turn * 16 + 16)
                steps.turn(number * (PAIRS * 2))
                for m in range(PAIRS):
                    pool.wait_ge(picked_ready, number * PAIRS + (m + 3))
                    part = [picked[:, m, :, n, :] for n in range(PARTS)]
                    to = xt[:, u, m * P:(m + 1) * P].rearrange("p (a d) -> p a d", a=2)
                    steps.done(nc.gpsimd.tensor_tensor(part[2], part[2], part[1], ALU.add))
                    steps.done(nc.gpsimd.tensor_tensor(part[2], part[2], part[0], ALU.add))
                    nc.gpsimd.tensor_tensor(to, to, part[2], ALU.add).then_inc(pair_added, 1)

            pool.wait_ge(bias_ready, 2)
            make_bias(1, 1, 0, 0)
            for half in range(HALVES):
                with pool.Fori(max(1, half * TURNS), (half + 1) * TURNS) as it:
                    for u in range(UN):
                        make_bias(it * UN + u, u, it, half)
                        add_pairs(it * UN + (u - UN), u, it - 1)
            for u in range(UN):
                add_pairs(HALVES * TILES - UN + u, u, HALVES * TURNS - 1)

        @block.tensor
        def _(pe):
            gate = Gate(pe, pe_passed)
            pe.sem_inc(turned_used, 4)
            pe.sem_inc(hits_turned, 2 * CHUNKS)
            pe.wait_ge(ident_ready, 2)

            def score_chunk(s, u, h, c, it, new_half):
                if c == 0 and h == 0:
                    pe.wait_ge(q_loaded[u], it * 32 + 32)
                if new_half and c == 0:
                    pe.wait_ge(k_loaded[h], new_half * 16)
                pe.wait_ge(scores_used, s * CHUNKS + (c + 1))
                for n in range(SC // 512):
                    keys = slice(c * SC + n * 512, c * SC + (n + 1) * 512)
                    for i in range(RPARTS):
                        last = nc.tensor.matmul(ps_s[:, c % 2, n * 512:(n + 1) * 512], q_sb[:, u, h, i, :],
                                                k_sb[:, h, keys], start=i == 0, stop=i == RPARTS - 1)
                last.then_inc(scores_ready, 1)

            def turn_chunk(s, h, c):
                if c == 0:
                    pe.wait_ge(hits_ready, s + 2)
                pe.wait_ge(turned_kept, s * CHUNKS + (c + 1))
                words = hits[:, h % 2, :].bitcast(F32)
                for b in range(TB):
                    at = (c * TB + b) * P
                    last = nc.tensor.transpose(ps_t[:, c % 2, b * P:(b + 1) * P], words[:, at:at + P], ident[:])
                last.then_inc(hits_turned, 1)

            def value_chunk(s, h, c, pair, new_half):
                if new_half and c == 0:
                    pe.wait_ge(v_loaded[h], new_half * 16)
                if c == 0 and h % 2 == 0:
                    pe.wait_ge(picked_ready, pair + 1)
                if c % 2 == 0:
                    gate.wait_ge(turned_kept, s * CHUNKS + (c + 4))
                a = h % 2
                to = ps_o[:, (h // 2) % 2, a * PARTS * HD:(a + 1) * PARTS * HD].rearrange("p (c d) -> p c d", c=PARTS)
                for b in range(TB):
                    for e in range(E):
                        last = nc.tensor.matmul(to, hitsT[:, c, b, :, e],
                                                v_sb[:, h, c * TB + b, e, :, :],
                                                start=a == 0 and c == 0 and b == 0 and e == 0,
                                                stop=c == CHUNKS - 1 and b == TB - 1 and e == E - 1,
                                                skip_group_check=True)
                last.then_inc(turned_used, 1)

            def turn(it, j, scored, valued, half=-1):
                s = it * (UN * HH) + j
                h = j % HH
                sv = s - LAG
                hv = (j - LAG) % HH
                pair = it * (UN * PAIRS) + (j - LAG) // 2
                new_keys = half + 1 if j < HH else 0
                new_values = half + 1 if LAG <= j < HH + LAG else 0
                for c in range(CHUNKS):
                    if valued:
                        turn_chunk(sv, hv, c)
                    if scored:
                        score_chunk(s, j // HH % UN, h, c, it, new_keys)
                    if valued and c % 2:
                        value_chunk(sv, hv, c - 1, pair, new_values)
                        value_chunk(sv, hv, c, pair, new_values)

            for half in range(HALVES):
                for j in range(UN * HH):
                    turn(half * TURNS, j, True, half > 0 or j >= LAG, half)
                with pe.Fori(half * TURNS + 1, (half + 1) * TURNS) as it:
                    for j in range(UN * HH):
                        turn(it, j, True, True)
            for j in range(LAG):
                turn(HALVES * TURNS, j, False, True)

        @block.scalar
        def _(act):
            act.sem_inc(turned_kept, 2)
            act.sem_inc(picked_ready, 2)
            def make_signs(t, u, turn, i):
                act.wait_ge(adj_loaded[i], t * 16 + 16)
                if not isinstance(turn, int):
                    act.wait_ge(signs_stored[u], turn * 16)
                nc.scalar.activation(signs[:, u, i * HN:(i + 1) * HN], adj_rows[:, i, :], ACT.Sign)\
                  .then_inc(signs_ready, 1)

            def turn(it, with_signs):
                for j in range(UN * HH):
                    s = it * (UN * HH) + j
                    for c in range(CHUNKS):
                        act.wait_ge(hits_turned, s * CHUNKS + (c + 1 + 2 * CHUNKS))
                        act.wait_ge(turned_used, s * CHUNKS + (c + 1))
                        nc.scalar.copy(hitsT[:, c, :, :, :].rearrange("p b q e -> p (b q e)").bitcast(U16),
                                       ps_t[:, c % 2, 0:TB * P].bitcast(U16)).then_inc(turned_kept, 1)
                    if j % 2:
                        pair = it * (UN * PAIRS) + j // 2
                        m = j // 2 % PAIRS
                        act.wait_ge(turned_used, s * CHUNKS + (CHUNKS + 4))
                        act.wait_ge(pair_added, pair + 1)
                        nc.scalar.mul(picked[:, m, :, :, :].rearrange("p a c d -> p (a c d)"),
                                      ps_o[:, m, 0:2 * PARTS * HD], 1.0 / HEADS).then_inc(picked_ready, 1)
                    if with_signs and j % HH >= HH // 2:
                        u = j // HH
                        make_signs(it * UN + (UN + u), u, it + 1, j % HH - HH // 2)

            for u in range(UN):
                for i in range(2):
                    make_signs(u, u, 0, i)
            with act.Fori(0, TURNS - 1) as it:
                turn(it, True)
            with act.Fori(TURNS - 1, HALVES * TURNS) as it:
                turn(it, False)

        @block.vector
        def _(v):
            v.sem_inc(scores_used, 2)
            steps = Steps(v, dve_step)
            gate = Gate(v, dve_passed)
            v.sem_inc(hits_ready, 1)
            for i in range(2):
                v.wait_ge(adj_loaded[i], 16)
                nc.vector.tensor_scalar(bias[:, 0, i * HN:(i + 1) * HN], adj_rows[:, i, :], 0.0, MASKED,
                                        ALU.is_le, ALU.mult).then_inc(bias_ready, 1)
            v.wait_ge(be_loaded, 16)
            with v.Fori(0, HALVES * TILES // UN) as it:
                for j in range(UN * HH):
                    u, h = j // HH, j % HH
                    s = it * (UN * HH) + j
                    if h == 0:
                        v.wait_ge(bias_ready, (it * UN + u) * 2 + 2)
                    v.wait_ge(hits_ready, s + 1)
                    for c in range(CHUNKS):
                        gate.wait_ge(scores_ready, s * CHUNKS + (c + 1))
                        at = slice(c * SC, (c + 1) * SC)
                        nc.vector.tensor_tensor_reduce(scores[:, at], ps_s[:, c % 2, :], bias[:, u, at], 1.0, FLOOR,
                                                       ALU.add, ALU.max, top[:, c:c + 1]).then_inc(scores_used, 1)
                    v.wait_ge(scores_used, s * CHUNKS + (CHUNKS + 2))
                    steps.turn(s * 2)
                    steps.done(nc.vector.reduce_max(least[:, 0:1], top[:], mybir.AxisListType.X))
                    steps.done(nc.vector.tensor_scalar(least[:, 1:2], least[:, 0:1], be_col[:, 0:1], TIE,
                                                       ALU.add, ALU.subtract))
                    gate.wait_ge(hits_turned, s * CHUNKS + CHUNKS)
                    nc.vector.tensor_scalar(hits[:, j % 2, :], scores[:], be_col[:, 0:1], least[:, 1:2],
                                            ALU.add, ALU.is_ge, saturate=False).then_inc(hits_ready, 1)


def layer1(nc, sem, adj_signs, x1_scr, u_scr, W_self, b_self, W_nb, b_nb, W_comb, b_comb, out):
    with ExitStack() as outer:
        g_sb = outer.enter_context(nc.sbuf_tensor("g_parts", [P, TILES, PARTS, D], BF16))
        ident = outer.enter_context(nc.sbuf_tensor("l_ident", [P, P], F32))
        linear_maps(nc, sem, x1_scr, u_scr, g_sb, ident, W_self, b_self, W_nb, b_nb, W_comb, b_comb)
        aggregation(nc, sem, x1_scr, adj_signs, u_scr, g_sb, ident, out)


def linear_maps(nc, sem, x1_scr, u_scr, g_sb, ident, W_self, b_self, W_nb, b_nb, W_comb, b_comb):
    UN = 2
    OUTS = 2 * GT
    assert GT == E
    x1_g = x1_scr.rearrange("(g j e) f -> g j (e f)", j=P, e=E)
    u_v = u_scr.rearrange("(g j e) f -> g e j f", j=P, e=E)
    with ExitStack() as ctx:
        def sb(name, shape, dt):
            return ctx.enter_context(nc.sbuf_tensor(name, shape, dt))

        spare = g_sb[:, 20:TILES, :, :].rearrange("p t c f -> p (t c f)").bitcast(F32)
        w_rows = sb("l_w_rows", [P, KC, D], F32)
        w_rowsT = sb("l_w_rowsT", [P, KC, D], F32)
        w_comb = sb("l_w_comb", [P, KC, D], F32)
        w_rows2, w_comb2 = (spare[:, i * KC * D:(i + 1) * KC * D].rearrange("p (c f) -> p c f", c=KC) for i in range(2))
        w = sb("l_w", [P, 2, KC, D], F32)
        b_cols = sb("l_b_cols", [P, 2 * KC], F32)
        b_wide = sb("l_b_wide", [P, 2 * KC, P], F32)
        b_row = sb("l_b_row", [P, D], F32)
        ones = sb("l_ones", [P, P], F32)
        xb = sb("l_x", [P, UN, GT, D], F32)
        xn = sb("l_xn", [P, GT, D], F32)
        hT = sb("l_hT", [P, UN, KC, GR], F32)
        stats = sb("l_stats", [P, GT, 6], F32)
        mv = sb("l_mv", [P, GT, 2], F32)
        small = sb("l_small", [P, 4, GT], F32)
        u_sb = sb("l_u", [P, 2, D], F32)
        value = sb("l_value", [P, 2, D], F32)
        rest = sb("l_rest", [P, D], F32)
        ps_t = ctx.enter_context(nc.psum_tensor("l_ps_t", [P, 2, D], F32))
        ps_o = ctx.enter_context(nc.psum_tensor("l_ps_o", [P, 4, D], F32))
        ps_b = ctx.enter_context(nc.psum_tensor("l_ps_b", [P, D], F32))

        ident_ready = sem("l_ident_ready")
        w_loaded = [sem(f"l_w_loaded{i}") for i in range(2)]
        b_loaded = sem("l_b_loaded")
        x_loaded = [sem(f"l_x_loaded{u}") for u in range(UN)]
        wide_ready = sem("l_wide_ready")
        bias_ready = sem("l_bias_ready")
        bias_kept = sem("l_bias_kept")
        var_ready = sem("l_var_ready")
        root_ready = sem("l_root_ready")
        xn_ready = sem("l_xn_ready")
        rows_turned = sem("l_rows_turned")
        turned_kept = sem("l_turned_kept")
        w_ready = sem("l_w_ready")
        w_kept = sem("l_w_kept")
        out_ready = sem("l_out_ready")
        value_ready = sem("l_value_ready")
        u_ready = sem("l_u_ready")
        value_split = sem("l_value_split")
        dve_step = sem("l_dve_step")
        u_stored = [sem(f"l_u_stored{a}") for a in range(2)]
        sp_passed = sem("l_sp_passed")
        dve_passed = sem("l_dve_passed")
        block = ctx.enter_context(nc.Block())

        W_FILLS = 2 * KC

        @block.gpsimd
        def _(pool):
            make_identity(nc, pool, ident, ident_ready)

        @block.sync
        def _(sp):
            sp_gate = Gate(sp, sp_passed)
            sp.dma_start(w_rows[:], W_self.rearrange("(c p) f -> p c f", p=P)).then_inc(w_loaded[0], 16)
            sp.dma_start(w_comb[:], W_comb[0:D, :].rearrange("(c p) f -> p c f", p=P)).then_inc(w_loaded[0], 16)
            sp.dma_start(xb[:, 0, :, :].rearrange("j e f -> j (e f)"), x1_g[0, :, :]).then_inc(x_loaded[0], 16)
            for i, b in enumerate((b_self, b_nb)):
                sp.dma_start(b_cols[:, i * KC:(i + 1) * KC], b.rearrange("(c p) -> p c", p=P),
                             allow_slow_non_contiguous=True).then_inc(b_loaded, 16)
            sp.dma_start(b_row[:], b_comb.rearrange("(a f) -> a f", a=1).broadcast_to([P, D])).then_inc(b_loaded, 16)
            for u in range(1, UN):
                sp.dma_start(xb[:, u, :, :].rearrange("j e f -> j (e f)"), x1_g[u, :, :])\
                  .then_inc(x_loaded[u], 16)
            sp.dma_start(w_rows2, W_nb.rearrange("(c p) f -> p c f", p=P)).then_inc(w_loaded[1], 16)
            sp.dma_start(w_comb2, W_comb[D:2 * D, :].rearrange("(c p) f -> p c f", p=P)).then_inc(w_loaded[1], 16)

            def group(g, u, last):
                if not last:
                    sp_gate.wait_ge(xn_ready, g + 1)
                    sp.dma_start(xb[:, u, :, :].rearrange("j e f -> j (e f)"), x1_g[g + 2, :, :])\
                      .then_inc(x_loaded[u], 16)
                for t in range(GT):
                    sp_gate.wait_ge(u_ready, g * GT + (t + 1))
                    sp.dma_start(u_v[g, t, :, :], u_sb[:, t % 2, :]).then_inc(u_stored[t % 2], 16)

            with sp.Fori(0, GROUPS // UN - 1) as it:
                for u in range(UN):
                    group(it * UN + u, u, False)
            for u in range(UN):
                group(GROUPS - UN + u, u, True)
            for a in range(2):
                sp_gate.wait_ge(u_stored[a], TILES // 2 * 16)

        @block.tensor
        def _(pe):
            pe.wait_ge(ident_ready, 2)

            def turn_rows(g):
                pe.wait_ge(xn_ready, g + 1)
                for k in range(KC):
                    pe.wait_ge(turned_kept, g * KC + (W_FILLS + k + 1))
                    for t in range(GT):
                        last = nc.tensor.transpose(ps_t[:, k % 2, t * P:(t + 1) * P],
                                                   xn[:, t, k * P:(k + 1) * P], ident[:])
                    last.then_inc(rows_turned, 1)

            for i, (rows, comb) in enumerate(((w_rows, w_comb), (w_rows2, w_comb2))):
                pe.wait_ge(w_loaded[i], 32)
                for k in range(KC):
                    f = i * KC + k
                    pe.wait_ge(turned_kept, f + 1)
                    for c in range(KC):
                        last = nc.tensor.transpose(ps_t[:, f % 2, c * P:(c + 1) * P],
                                                   rows[:, c, k * P:(k + 1) * P], ident[:])
                    last.then_inc(rows_turned, 1)
                if i == 0:
                    pe.wait_ge(wide_ready, 2 * KC)
                for k in range(KC):
                    last = nc.tensor.matmul(ps_b[:], b_wide[:, i * KC + k, :], comb[:, k, :],
                                            start=i == 0 and k == 0, stop=i == 1 and k == KC - 1,
                                            skip_group_check=True)
                if i == 1:
                    last.then_inc(bias_ready, 1)
                pe.wait_ge(turned_kept, i * KC + KC + 2)
                for c in range(KC):
                    if i == 1:
                        pe.wait_ge(w_kept, c + 1)
                    for k in range(KC):
                        last = nc.tensor.matmul(ps_o[:, c, :], w_rowsT[:, k, c * P:(c + 1) * P], comb[:, k, :],
                                                start=k == 0, stop=k == KC - 1)
                    last.then_inc(w_ready, 1)

            def group(g, u, last_group):
                pe.wait_ge(turned_kept, g * KC + (W_FILLS + KC + 2))
                for o in range(OUTS):
                    t, i = o // 2, o % 2
                    if t < 2:
                        if not isinstance(g, int) or g > 0:
                            pe.wait_ge((u_ready, value_ready)[i], g * GT + (t - 1))
                    else:
                        pe.wait_ge((u_ready, value_ready)[i], g * GT + (t - 1))
                    for k in range(KC):
                        last = nc.tensor.matmul(ps_o[:, o % 4, :], hT[:, u, k, t * P:(t + 1) * P], w[:, i, k, :],
                                                start=k == 0, stop=k == KC - 1)
                    last.then_inc(out_ready, 1)
                    if o == 5 and not last_group:
                        turn_rows(g + 1)

            turn_rows(0)
            pe.wait_ge(w_kept, 2 * KC)
            group(0, 0, False)
            group(1, 1, False)
            with pe.Fori(1, GROUPS // UN - 1) as it:
                for u in range(UN):
                    group(it * UN + u, u, False)
            for u in range(UN):
                group(GROUPS - UN + u, u, u == UN - 1)

        @block.scalar
        def _(act):
            act.sem_inc(turned_kept, 2)
            for i in range(2):
                if i == 1:
                    act.wait_ge(w_ready, KC)
                for k in range(KC):
                    f = i * KC + k
                    act.wait_ge(rows_turned, f + 1)
                    nc.scalar.copy(w_rowsT[:, k, :], ps_t[:, f % 2, :]).then_inc(turned_kept, 1)
                for c in range(KC):
                    act.wait_ge(w_ready, i * KC + c + 1)
                    nc.scalar.copy(w[:, i, c, :], ps_o[:, c, :]).then_inc(w_kept, 1)

            def root(g):
                act.wait_ge(var_ready, g + 1)
                nc.scalar.activation(small[:, 1, :], small[:, 0, :], ACT.Sqrt).then_inc(root_ready, 1)

            def keep_rows(g, u):
                for k in range(KC):
                    act.wait_ge(rows_turned, g * KC + (W_FILLS + k + 1))
                    nc.scalar.activation(hT[:, u, k, :], ps_t[:, k % 2, :], ACT.Relu).then_inc(turned_kept, 1)

            def group(g, u, last_group):
                for t in range(GT):
                    if t == 1 and not last_group:
                        root(g + 1)
                    act.wait_ge(out_ready, g * OUTS + (2 * t + 2))
                    if t >= 2 or not isinstance(g, int) or g > 0:
                        act.wait_ge(value_split, g * GT + (t - 1))
                    nc.scalar.copy(value[:, t % 2, :], ps_o[:, 2 * (t % 2) + 1, :]).then_inc(value_ready, 1)
                    if t == 2 and not last_group:
                        keep_rows(g + 1, 1 - u)

            root(0)
            keep_rows(0, 0)
            group(0, 0, False)
            group(1, 1, False)
            with act.Fori(1, GROUPS // UN - 1) as it:
                for u in range(UN):
                    group(it * UN + u, u, False)
            for u in range(UN):
                group(GROUPS - UN + u, u, u == UN - 1)

        @block.vector
        def _(v):
            steps = Steps(v, dve_step)
            steps.done(nc.vector.memset(ones[:], 1.0))
            v.wait_ge(b_loaded, 3 * 16)
            for c in range(2 * KC):
                nc.vector.tensor_scalar(b_wide[:, c, :], ones[:], b_cols[:, c:c + 1], None, ALU.mult)\
                  .then_inc(wide_ready, 1)
            NORM = NORM_STEPS - 2
            PER = GT * SPLIT_STEPS + NORM

            def norm(g, u, it):
                v.wait_ge(x_loaded[u], it * 16 + 16)
                if not isinstance(g, int) or g > 0:
                    v.wait_ge(turned_kept, g * KC + (W_FILLS + 2))
                normalise(nc, v, Gate(v, dve_passed), steps, xb[:, u], xn, stats, mv, small, var_ready, root_ready, g)\
                    .then_inc(xn_ready, 1)

            def group(g, u, it, last_group):
                steps.turn(g * PER + (NORM + 1))
                for t in range(GT):
                    v.wait_ge(out_ready, g * OUTS + (2 * t + 1))
                    if not isinstance(g, int) or g * GT + t >= 2:
                        v.wait_ge(u_stored[t % 2], (g * 2 + t // 2) * 16)
                    nc.vector.tensor_tensor(u_sb[:, t % 2, :], ps_o[:, 2 * (t % 2), :], b_row[:], ALU.add)\
                      .then_inc(u_ready, 1)
                    v.wait_ge(value_ready, g * GT + (t + 1))
                    parts = [g_sb[:, bass.ds(g * GT + t, 1), n, :].rearrange("p a f -> p (a f)") for n in range(PARTS)]
                    split(nc, steps, value[:, t % 2, :], rest[:], *parts).then_inc(value_split, 1)
                    if t == 0 and not last_group:
                        norm(g + 1, 1 - u, it + u)

            norm(0, 0, 0)
            v.wait_ge(bias_ready, 1)
            nc.vector.tensor_tensor(b_row[:], ps_b[:], b_row[:], ALU.add).then_inc(bias_kept, 1)
            v.wait_ge(bias_kept, 1)
            group(0, 0, 0, False)
            group(1, 1, 0, False)
            with v.Fori(1, GROUPS // UN - 1) as it:
                for u in range(UN):
                    group(it * UN + u, u, it, False)
            for u in range(UN):
                group(GROUPS - UN + u, u, GROUPS // UN - 1, u == UN - 1)


def aggregation(nc, sem, x1_scr, sign_scr, u_scr, g_sb, ident, out):
    UN = 2
    x1_v, u_v, out_v = (a.rearrange("(b u p) f -> b u p f", u=UN, p=P) for a in (x1_scr, u_scr, out))
    sign_v = sign_scr.rearrange("(b u) p k -> b u p k", u=UN)
    with ExitStack() as ctx:
        def sb(name, shape, dt):
            return ctx.enter_context(nc.sbuf_tensor(name, shape, dt))

        signs = sb("g_signs", [P, UN, N], I8)
        mask = sb("g_mask", [P, UN, N], F8)
        maskT = sb("g_maskT", [P, UN, BLOCKS, P, E], F8)
        deg = sb("g_deg", [P, UN, 3], F32)
        u_sb = sb("g_u", [P, UN, D], F32)
        x1 = sb("g_x1", [P, UN, D], F32)
        mixed = sb("g_mixed", [P, D], F32)
        y = sb("g_y", [P, UN, D], F32)
        ps_t = ctx.enter_context(nc.psum_tensor("g_ps_t", [P, 2, 512], F32))
        ps_o = ctx.enter_context(nc.psum_tensor("g_ps_o", [P, 2, D], F32))

        signs_loaded = [sem(f"g_signs_loaded{u}") for u in range(UN)]
        rows_loaded = [sem(f"g_rows_loaded{u}") for u in range(UN)]
        mask_ready = sem("g_mask_ready")
        deg_ready = sem("g_deg_ready")
        mask_turned = sem("g_mask_turned")
        turned_kept = sem("g_turned_kept")
        sum_ready = sem("g_sum_ready")
        sum_used = sem("g_sum_used")
        y_ready = sem("g_y_ready")
        y_stored = [sem(f"g_y_stored{u}") for u in range(UN)]
        sp_passed = sem("g_sp_passed")
        dve_passed = sem("g_dve_passed")
        pe_passed = sem("g_pe_passed")
        block = ctx.enter_context(nc.Block())

        @block.sync
        def _(sp):
            sp_gate = Gate(sp, sp_passed)
            def load_signs(b, u):
                sp.dma_start(signs[:, u, :], sign_v[b, u, :, :]).then_inc(signs_loaded[u], 16)

            def load_rows(b, u):
                sp.dma_start(u_sb[:, u, :], u_v[b, u, :, :]).then_inc(rows_loaded[u], 16)
                sp.dma_start(x1[:, u, :], x1_v[b, u, :, :]).then_inc(rows_loaded[u], 16)

            def store(b, u):
                sp_gate.wait_ge(y_ready, b * 2 + (u + 1))
                sp.dma_start(out_v[b, u, :, :], y[:, u, :]).then_inc(y_stored[u], 16)

            for u in range(UN):
                load_signs(0, u)
            for u in range(UN):
                load_rows(0, u)
            with sp.Fori(1, TILES // UN) as b:
                for u in range(UN):
                    sp_gate.wait_ge(mask_ready, b * 2 + (u - 1))
                    load_signs(b, u)
                    store(b - 1, u)
                    load_rows(b, u)
            for u in range(UN):
                store(TILES // UN - 1, u)
            for u in range(UN):
                sp_gate.wait_ge(y_stored[u], TILES // UN * 16)

        @block.tensor
        def _(pe):
            gate = Gate(pe, pe_passed)

            def turn_chunk(n, u, c):
                if c == 0:
                    pe.wait_ge(mask_ready, n + 1)
                pe.wait_ge(turned_kept, n * CHUNKS + (c + 1))
                words = mask[:, u, :].bitcast(F32)
                for b in range(TB):
                    at = (c * TB + b) * P
                    last = nc.tensor.transpose(ps_t[:, c % 2, b * P:(b + 1) * P], words[:, at:at + P], ident[:])
                last.then_inc(mask_turned, 1)

            def sum_chunk(n, u, c):
                if c == 0:
                    pe.wait_ge(sum_used, n + 1)
                    gate.wait_ge(turned_kept, n * CHUNKS + (CHUNKS + 2))
                for b in range(c * TB, (c + 1) * TB):
                    for e in range(E):
                        for part in range(PARTS):
                            last = nc.tensor.matmul(ps_o[:, u, :], maskT[:, u, b, :, e], g_sb[:, E * b + e, part, :],
                                                    start=b == 0 and e == 0 and part == 0,
                                                    stop=b == BLOCKS - 1 and e == E - 1 and part == PARTS - 1)
                if c == CHUNKS - 1:
                    last.then_inc(sum_ready, 1)

            def tile(n, u, last):
                for c in range(CHUNKS):
                    sum_chunk(n, u, c)
                    if not last and c < CHUNKS - 1:
                        turn_chunk(n + 1, 1 - u, c)
                        if c == CHUNKS - 2:
                            turn_chunk(n + 1, 1 - u, CHUNKS - 1)

            for c in range(CHUNKS):
                turn_chunk(0, 0, c)
            with pe.Fori(0, TILES // UN - 1) as b:
                for u in range(UN):
                    tile(b * 2 + u, u, False)
            for u in range(UN):
                tile(TILES - UN + u, u, u == UN - 1)

        @block.scalar
        def _(act):
            act.sem_inc(turned_kept, 2)

            def keep(n, u, b):
                if not isinstance(b, int) or b > 0:
                    act.wait_ge(sum_ready, n - 1)
                for c in range(CHUNKS):
                    act.wait_ge(mask_turned, n * CHUNKS + (c + 1))
                    nc.scalar.copy(maskT[:, u, c * TB:(c + 1) * TB, :, :].rearrange("p b q e -> p (b q e)").bitcast(U16),
                                   ps_t[:, c % 2, 0:TB * P].bitcast(U16)).then_inc(turned_kept, 1)

            for u in range(UN):
                keep(u, u, 0)
            with act.Fori(1, TILES // UN) as b:
                for u in range(UN):
                    keep(b * 2 + u, u, b)

        @block.vector
        def _(v):
            v.sem_inc(sum_used, 2)
            gate = Gate(v, dve_passed)

            def masks(n, u, b):
                v.wait_ge(signs_loaded[u], b * 16 + 16)
                if not isinstance(n, int) or n >= 2:
                    gate.wait_ge(mask_turned, (n - 1) * CHUNKS)
                nc.vector.tensor_scalar(mask[:, u, :], signs[:, u, :], 0.0, 0.0, ALU.is_gt, ALU.add,
                                        accum_out=deg[:, u, 0:1], saturate=False).then_inc(mask_ready, 1)
                v.wait_ge(mask_ready, n + 1)
                nc.vector.tensor_scalar(deg[:, u, 1:2], deg[:, u, 0:1], 1.0, None, ALU.max).then_inc(deg_ready, 1)
                v.wait_ge(deg_ready, n * 2 + 1)
                nc.vector.reciprocal(deg[:, u, 2:3], deg[:, u, 1:2]).then_inc(deg_ready, 1)

            def finish(n, u, b):
                if not isinstance(n, int) or n > 0:
                    v.wait_ge(y_ready, n)
                v.wait_ge(sum_ready, n + 1)
                v.wait_ge(rows_loaded[u], b * 32 + 32)
                v.wait_ge(deg_ready, n * 2 + 2)
                nc.vector.scalar_tensor_tensor(mixed[:], ps_o[:, u, :], deg[:, u, 2:3], u_sb[:, u, :],
                                               ALU.mult, ALU.add).then_inc(sum_used, 1)
                v.wait_ge(sum_used, n + 3)
                if not isinstance(b, int) or b > 0:
                    v.wait_ge(y_stored[u], b * 16)
                nc.vector.scalar_tensor_tensor(y[:, u, :], mixed[:], 0.0, x1[:, u, :],
                                               ALU.max, ALU.add).then_inc(y_ready, 1)

            masks(0, 0, 0)
            masks(1, 1, 0)
            finish(0, 0, 0)
            with v.Fori(1, TILES // UN) as b:
                masks(b * 2, 0, b)
                finish(b * 2 - 1, 1, b - 1)
                masks(b * 2 + 1, 1, b)
                finish(b * 2, 0, b)
            finish(TILES - 1, 1, TILES // UN - 1)


def two_layers(nc, x, adj, WQ, WK, WV, we, be, W_self, b_self, W_nb, b_nb, W_comb, b_comb, out):
    def scratch(name, shape, dt):
        return nc.dram_tensor(name, shape, dt).ap()

    q_scr = scratch("q_scr", [HEADS, RPARTS, HD, N], F32)
    k_scr = scratch("k_scr", [HEADS, RPARTS * HD, N], F32)
    v_scr = scratch("v_scr", [HEADS, N, PARTS, HD], BF16)
    sign_scr = scratch("sign_scr", [TILES, P, N], I8)
    x1_scr = scratch("x1_scr", [N, D], F32)
    u_scr = scratch("u_scr", [N, D], F32)
    with ExitStack() as sems:
        def sem(name):
            return sems.enter_context(nc.semaphore(name))

        projections(nc, sem, x, WQ, WK, WV, we, q_scr, k_scr, v_scr)
        attention(nc, sem, x, adj, be, q_scr, k_scr, v_scr, sign_scr, x1_scr)
        layer1(nc, sem, sign_scr, x1_scr, u_scr, W_self, b_self, W_nb, b_nb, W_comb, b_comb, out)


_INS = ["x", "adj", "L0_gnn_WQ", "L0_gnn_WK", "L0_gnn_WV", "L0_gnn_we", "L0_gnn_be",
        "L1_gnn_W_self", "L1_gnn_b_self", "L1_gnn_W_nb", "L1_gnn_b_nb", "L1_gnn_W_comb", "L1_gnn_b_comb"]


def kernel(**inputs):
    import numpy as _np
    import concourse.bacc as _bacc
    from concourse import mybir as _mybir
    from concourse.bass_utils import run_bass_kernel_spmd as _run

    nc = _bacc.Bacc("TRN2", target_bir_lowering=False, num_devices=1)
    arrays, args = {}, []
    for name in _INS:
        a = _np.ascontiguousarray(inputs[name])
        arrays[f"in_{name}_dram"] = a
        args.append(nc.dram_tensor(f"in_{name}_dram", a.shape, _mybir.dt.from_np(a.dtype), kind="ExternalInput").ap())
    args.append(nc.dram_tensor("out_0_dram", (N, D), F32, kind="ExternalOutput").ap())
    two_layers(nc, *args)
    r = _run(nc, [arrays], core_ids=[0])
    return r.results[0]["out_0_dram"]
```

```python
from contextlib import ExitStack

import concourse.bass as bass
from concourse import mybir

F32 = mybir.dt.float32
BF16 = mybir.dt.bfloat16
F32R = mybir.dt.float32r
I8 = mybir.dt.int8
U16 = mybir.dt.uint16
F8 = mybir.dt.float8e4
I32 = mybir.dt.int32
ALU = mybir.AluOpType
ACT = mybir.ActivationFunctionType

P = 128
N = 4096
D = 512
HEADS = 8
HD = D // HEADS
KC = D // P
TILES = N // P
GT = 4
GROUPS = TILES // GT
GR = GT * P
PARTS = 3
RPARTS = 2
E = 4
BLOCKS = N // (E * P)
EPS = 1e-5
SCALING = HD ** -0.5
HH = 4
HALF = HH * HD
SC = 1024
CHUNKS = N // SC
HN = N // 2
TB = BLOCKS // CHUNKS
MASKED = -1e30
FLOOR = -1e29
LOWEST = -3e38
TIE = 2.0 ** -25


class Steps:

    def __init__(self, engine, sem):
        self.engine, self.sem, self.base, self.n = engine, sem, 0, 0

    def turn(self, base):
        self.base, self.n = base, 0

    def done(self, instruction):
        self.n += 1
        instruction.then_inc(self.sem, 1)
        self.engine.wait_ge(self.sem, self.base + self.n)


class Gate:

    def __init__(self, engine, sem):
        self.engine, self.sem = engine, sem

    def wait_ge(self, sem, value):
        self.engine.wait_ge(sem, value)
        self.engine.sem_inc(self.sem, 1)


def make_identity(nc, pool, ident, sem):
    nc.gpsimd.memset(ident[:], 0.0).then_inc(sem, 1)
    pool.wait_ge(sem, 1)
    nc.gpsimd.affine_select(out=ident[:], in_=ident[:], compare_op=ALU.not_equal, fill=1.0, base=0,
                            pattern=[[-1, P]], channel_multiplier=1).then_inc(sem, 1)


NORM_STEPS = 2 * GT + 7


def normalise(nc, v, gate, steps, x, xn, stats, mv, small, var_ready, root_ready, turn):
    for t in range(GT):
        nc.vector.bn_stats(stats[:, t, :], x[:, t, :]).then_inc(steps.sem, 1)
        steps.n += 1
    gate.wait_ge(steps.sem, steps.base + steps.n)
    for t in range(GT):
        nc.vector.bn_aggr(mv[:, t, :], stats[:, t, :]).then_inc(steps.sem, 1)
        steps.n += 1
    v.wait_ge(steps.sem, steps.base + steps.n)
    var, root, inv, other = (small[:, i, :] for i in range(4))
    nc.vector.tensor_scalar(var, mv[:, :, 1], EPS, None, ALU.add).then_inc(var_ready, 1)
    v.wait_ge(root_ready, turn + 1)
    steps.done(nc.vector.reciprocal(inv, root))
    steps.done(nc.vector.tensor_tensor(other, var, inv, ALU.mult))
    steps.done(nc.vector.tensor_tensor(other, other, root, ALU.add))
    steps.done(nc.vector.tensor_scalar(other, other, 0.5, None, ALU.mult))
    steps.done(nc.vector.reciprocal(inv, other))
    for t in range(GT):
        last = nc.vector.tensor_scalar(xn[:, t, :], x[:, t, :], mv[:, t, 0:1], inv[:, t:t + 1],
                                       ALU.subtract, ALU.mult)
    return last


SPLIT_STEPS = 3


def split(nc, steps, value, rest, high, middle, low):
    steps.done(nc.vector.tensor_copy(high, value))
    steps.done(nc.vector.tensor_tensor(rest, value, high, ALU.subtract))
    steps.done(nc.vector.tensor_copy(middle, rest))
    return nc.vector.tensor_tensor(low, rest, middle, ALU.subtract)


def projections(nc, sem, x, WQ, WK, WV, we, q_scr, k_scr, v_scr, v_stored,
                adj, adj_rows, adj_loaded):
    x_v = x.rearrange("(g t p) f -> g p t f", t=GT, p=P)
    v_v = v_scr.rearrange("h (g t p) c f -> g t p h (c f)", t=GT, p=P)
    UN = 2
    OUTS = 3 * KC
    STORES = 2 * RPARTS
    NORM_AT = 0
    ROOT_AT = 1
    ROWS_AT = 4
    WEIGHTS_AT = (2, 3)

    with ExitStack() as ctx:
        def sb(name, shape, dt):
            return ctx.enter_context(nc.sbuf_tensor(name, shape, dt))

        ident = sb("p_ident", [P, P], F32)
        w_rows = sb("p_w_rows", [P, 3, KC, D], F32)
        wT = sb("p_wT", [P, 3, RPARTS, KC, D], F32R)
        v_parts = sb("p_v_parts", [P, GT, HEADS, PARTS, HD], BF16)
        we_col = sb("p_we_col", [P, 1], F32)
        xb = sb("p_x", [P, UN, GT, D], F32)
        xn = sb("p_xn", [P, GT, D], F32)
        hT = sb("p_hT", [P, UN, RPARTS, KC, GR], F32R)
        stats = sb("p_stats", [P, GT, 6], F32)
        mv = sb("p_mv", [P, GT, 2], F32)
        small = sb("p_small", [P, 4, GT], F32)
        value = sb("p_value", [P, 2, D], F32)
        rest = sb("p_rest", [P, D], F32)
        k_parts = sb("p_k_parts", [P, RPARTS, KC, GR], F32R)
        q_parts = sb("p_q_parts", [P, RPARTS, KC, GR], F32R)
        ps_t = ctx.enter_context(nc.psum_tensor("p_ps_t", [P, 2, D], F32))
        ps_o = ctx.enter_context(nc.psum_tensor("p_ps_o", [P, 4, D], F32))

        w_loaded = [sem(f"p_w_loaded{i}") for i in range(3)]
        we_loaded = sem("p_we_loaded")
        ident_ready = sem("p_ident_ready")
        x_loaded = [sem(f"p_x_loaded{u}") for u in range(UN)]
        var_ready = sem("p_var_ready")
        root_ready = sem("p_root_ready")
        xn_ready = sem("p_xn_ready")
        rows_turned = sem("p_rows_turned")
        turned_high = sem("p_turned_high")
        turned_kept = sem("p_turned_kept")
        out_ready = sem("p_out_ready")
        value_ready = sem("p_value_ready")
        high_ready = sem("p_high_ready")
        value_split = sem("p_value_split")
        dve_step = sem("p_dve_step")
        k_stored = sem("p_k_stored")
        q_stored = sem("p_q_stored")
        sp_passed = sem("p_sp_passed")
        dve_passed = sem("p_dve_passed")
        block = ctx.enter_context(nc.Block())

        W_FILLS = 3 * KC

        def weights_bank(i, k):
            return i * KC + k + (KC if i else 0)

        def rows_bank(g, k):
            return KC + k if isinstance(g, int) and g == 0 else g * KC + (W_FILLS + k)

        PRODUCTS = ((0, 0), (0, 1), (1, 0))

        @block.gpsimd
        def _(pool):
            make_identity(nc, pool, ident, ident_ready)

        @block.sync
        def _(sp):
            sp_gate = Gate(sp, sp_passed)
            for i, w in enumerate((WK, WQ, WV)):
                if i < UN:
                    sp.dma_start(xb[:, i, :, :], x_v[i, :, :, :]).then_inc(x_loaded[i], 16)
                sp.dma_start(w_rows[:, i, :, :], w.rearrange("(c p) f -> p c f", p=P)).then_inc(w_loaded[i], 16)
            for a in range(2):
                sp.dma_start(we_col[a * HD:(a + 1) * HD, :], we.rearrange("a d -> d a")).then_inc(we_loaded, 16)
            for i in range(2):
                sp.dma_start(adj_rows[:, i, :], adj[0:P, i * HN:(i + 1) * HN]).then_inc(adj_loaded[i], 16)

            def group(g, u, last_x):
                for t in range(1, GT):
                    if t == 1:
                        sp_gate.wait_ge(value_split, g * OUTS + (2 + KC))
                        for part in range(RPARTS):
                            for a in range(2):
                                sp.dma_start(
                                    k_scr[a::2, part * HD:(part + 1) * HD, bass.ts(g, GR)].rearrange("c p r -> p c r"),
                                    k_parts[a * HD:(a + 1) * HD, part, :, :].bitcast(F32)).then_inc(k_stored, 16)
                    if t == 2:
                        sp_gate.wait_ge(value_split, g * OUTS + (2 + 2 * KC))
                        for part in range(RPARTS):
                            for a in range(2):
                                sp.dma_start(
                                    q_scr[a::2, part, :, bass.ts(g, GR)].rearrange("c p r -> p c r"),
                                    q_parts[a * HD:(a + 1) * HD, part, :, :].bitcast(F32)).then_inc(q_stored, 16)
                    if t == 3:
                        if not last_x:
                            sp_gate.wait_ge(xn_ready, g + 1)
                            sp.dma_start(xb[:, u, :, :], x_v[g + 2, :, :, :]).then_inc(x_loaded[u], 16)
                        for i in range(GT):
                            sp_gate.wait_ge(value_split, g * OUTS + (2 * KC + i + 3))
                            sp.dma_start(v_v[g, i, :, :, :], v_parts[:, i, :, :, :].rearrange("p h c d -> p h (c d)"))\
                              .then_inc(v_stored, 16)

            with sp.Fori(0, GROUPS // UN - 1) as it:
                for u in range(UN):
                    group(it * UN + u, u, False)
            for u in range(UN):
                group(GROUPS - UN + u, u, True)
            sp_gate.wait_ge(k_stored, GROUPS * STORES * 16)
            sp_gate.wait_ge(q_stored, GROUPS * STORES * 16)

        @block.tensor
        def _(pe):
            pe.wait_ge(ident_ready, 2)

            def turn_weights(i):
                pe.wait_ge(w_loaded[i], 16)
                for k in range(KC):
                    n = weights_bank(i, k)
                    pe.wait_ge(turned_kept, n + 1)
                    for c in range(KC):
                        last = nc.tensor.transpose(ps_t[:, n % 2, c * P:(c + 1) * P],
                                                   w_rows[:, i, c, k * P:(k + 1) * P], ident[:])
                    last.then_inc(rows_turned, 1)

            def turn_rows(g, banks):
                pe.wait_ge(xn_ready, g + 1)
                for k in banks:
                    pe.wait_ge(turned_kept, rows_bank(g, k) + 1)
                    for t in range(GT):
                        last = nc.tensor.transpose(ps_t[:, k % 2, t * P:(t + 1) * P],
                                                   xn[:, t, k * P:(k + 1) * P], ident[:])
                    last.then_inc(rows_turned, 1)

            def group(g, u, last_group=False, first=False):
                pe.wait_ge(turned_kept, rows_bank(g, KC) + 2)
                for o in range(OUTS):
                    pe.wait_ge(value_ready, g * OUTS + (o + 1))
                    i, c = o // KC, o % KC
                    if first and c == 0 and i > 0:
                        pe.wait_ge(turned_kept, weights_bank(i, KC) + 2)
                    for k in range(KC):
                        for n, (a, b) in enumerate(PRODUCTS):
                            if i < 2:
                                lhsT, rhs = wT[:, i, a, k, c * P:(c + 1) * P], hT[:, u, b, k, :]
                            else:
                                lhsT, rhs = hT[:, u, b, k, c * P:(c + 1) * P], wT[:, i, a, k, :]
                            last = nc.tensor.matmul(ps_o[:, o % 4, :], lhsT, rhs, start=k == 0 and n == 0,
                                                    stop=k == KC - 1 and n == len(PRODUCTS) - 1)
                    last.then_inc(out_ready, 1)
                    if first and o in WEIGHTS_AT:
                        turn_weights(WEIGHTS_AT.index(o) + 1)
                    if 0 <= o - ROWS_AT < KC and not last_group:
                        turn_rows(g + 1, [o - ROWS_AT])

            turn_weights(0)
            turn_rows(0, range(KC))
            group(0, 0, first=True)
            group(1, 1)
            with pe.Fori(1, GROUPS // UN - 1) as it:
                for u in range(UN):
                    group(it * UN + u, u)
            for u in range(UN):
                group(GROUPS - UN + u, u, u == UN - 1)

        @block.scalar
        def _(act):
            act.sem_inc(value_ready, 4)

            def keep_weights(i):
                for k in range(KC):
                    n = weights_bank(i, k)
                    act.wait_ge(rows_turned, n + 1)
                    nc.scalar.copy(wT[:, i, 0, k, :], ps_t[:, n % 2, :]).then_inc(turned_high, 1)

            def root(g):
                act.wait_ge(var_ready, g + 1)
                nc.scalar.activation(small[:, 1, :], small[:, 0, :], ACT.Sqrt).then_inc(root_ready, 1)

            def keep_rows(g, u, banks):
                for k in banks:
                    act.wait_ge(rows_turned, rows_bank(g, k) + 1)
                    nc.scalar.activation(hT[:, u, 0, k, :], ps_t[:, k % 2, :], ACT.Relu).then_inc(turned_high, 1)

            def group(g, u, last_group=False, first=False):
                for o in range(OUTS):
                    i, c = o // KC, o % KC
                    act.wait_ge(out_ready, g * OUTS + (o + 1))
                    act.wait_ge(value_split, g * OUTS + (o + 1))
                    if i == 0:
                        nc.scalar.activation(value[:, o % 2, :], ps_o[:, o % 4, :], ACT.Identity,
                                             bias=we_col[:, 0:1], scale=SCALING).then_inc(value_ready, 1)
                    else:
                        nc.scalar.copy(value[:, o % 2, :], ps_o[:, o % 4, :]).then_inc(value_ready, 1)
                    if i < 2:
                        if c == 0 and not first:
                            act.wait_ge((k_stored, q_stored)[i], g * (STORES * 16))
                        act.wait_ge(value_ready, g * OUTS + (o + 5))
                        nc.scalar.copy((k_parts, q_parts)[i][:, 0, c, :], value[:, o % 2, :]).then_inc(high_ready, 1)
                    if o == ROOT_AT and not last_group:
                        root(g + 1)
                    if first and o in WEIGHTS_AT:
                        keep_weights(WEIGHTS_AT.index(o) + 1)
                    if 0 <= o - ROWS_AT < KC and not last_group:
                        keep_rows(g + 1, 1 - u, [o - ROWS_AT])

            root(0)
            keep_weights(0)
            act.wait_ge(we_loaded, 32)
            keep_rows(0, 0, range(KC))
            group(0, 0, first=True)
            group(1, 1)
            with act.Fori(1, GROUPS // UN - 1) as it:
                for u in range(UN):
                    group(it * UN + u, u)
            for u in range(UN):
                group(GROUPS - UN + u, u, u == UN - 1)

        @block.vector
        def _(v):
            v.sem_inc(value_split, 2)
            v.sem_inc(turned_kept, 2)
            steps = Steps(v, dve_step)
            NORM = NORM_STEPS - 2
            PER = KC * SPLIT_STEPS + NORM

            def keep_weights(i):
                for k in range(KC):
                    n = weights_bank(i, k)
                    v.wait_ge(turned_high, n + 1)
                    nc.vector.tensor_tensor(wT[:, i, 1, k, :], ps_t[:, n % 2, :], wT[:, i, 0, k, :].bitcast(F32),
                                            ALU.subtract).then_inc(turned_kept, 1)

            def keep_rows(g, u, banks):
                for k in banks:
                    v.wait_ge(turned_high, rows_bank(g, k) + 1)
                    nc.vector.scalar_tensor_tensor(hT[:, u, 1, k, :], ps_t[:, k % 2, :], 0.0,
                                                   hT[:, u, 0, k, :].bitcast(F32), ALU.max, ALU.subtract)\
                      .then_inc(turned_kept, 1)

            def norm(g, u, it):
                v.wait_ge(x_loaded[u], it * 16 + 16)
                if not isinstance(g, int) or g > 0:
                    v.wait_ge(turned_kept, rows_bank(0, KC) + 2 if isinstance(g, int) and g == 1
                              else g * KC + (W_FILLS + 2))
                normalise(nc, v, Gate(v, dve_passed), steps, xb[:, u], xn, stats, mv, small, var_ready, root_ready, g)\
                    .then_inc(xn_ready, 1)

            def group(g, u, it, last_group=False, first=False):
                steps.turn(g * PER + NORM)
                for o in range(OUTS):
                    i, c = o // KC, o % KC
                    if c == 0 and not first:
                        v.wait_ge((k_stored, q_stored, v_stored)[i], g * ((STORES, STORES, GT)[i] * 16))
                    if i < 2:
                        v.wait_ge(high_ready, g * (2 * KC) + (o + 1))
                        to = (k_parts, q_parts)[i]
                        last = nc.vector.tensor_tensor(to[:, 1, c, :], value[:, o % 2, :], to[:, 0, c, :].bitcast(F32),
                                                       ALU.subtract)
                    else:
                        v.wait_ge(value_ready, g * OUTS + (o + 5))
                        whole, left = (a.rearrange("p (h d) -> p h d", d=HD) for a in (value[:, o % 2, :], rest[:]))
                        last = split(nc, steps, whole, left, *(v_parts[:, c, :, n, :] for n in range(PARTS)))
                    last.then_inc(value_split, 1)
                    if first and o in WEIGHTS_AT:
                        keep_weights(WEIGHTS_AT.index(o) + 1)
                    if o == NORM_AT and not last_group:
                        norm(g + 1, 1 - u, it + u)
                    if 0 <= o - ROWS_AT < KC and not last_group:
                        keep_rows(g + 1, 1 - u, [o - ROWS_AT])

            steps.turn(0)
            norm(0, 0, 0)
            assert steps.n == NORM, steps.n
            keep_weights(0)
            keep_rows(0, 0, range(KC))
            group(0, 0, 0, first=True)
            assert steps.n == PER, steps.n
            group(1, 1, 0)
            with v.Fori(1, GROUPS // UN - 1) as it:
                for u in range(UN):
                    group(it * UN + u, u, it)
            for u in range(UN):
                group(GROUPS - UN + u, u, GROUPS // UN - 1, u == UN - 1)


def attention(nc, sem, x, adj, adj_rows, adj_loaded, be, q_scr, k_scr, v_scr, v_stored, sign_scr, x1_scr):
    n_ = "a_"
    HALVES = HEADS // HH
    v_v = v_scr.rearrange("h (b j e) c d -> h j b (e c d)", j=P, e=E)
    adj_v = adj.rearrange("(t p) k -> t p k", p=P)
    x_v = x.rearrange("(t p) f -> t p f", p=P)
    x1_v = x1_scr.rearrange("(t p) f -> t p f", p=P)
    UN = 2
    TURN_LAG = 2
    LAG = 3
    PLACE, BACK = (0, 1, 2, 1), (4, 2, 4, 2)
    ORDER = ((0, 1, 2, 3), (1, 2, 3, 0))
    TILE_CHUNKS = HH * CHUNKS
    PAIRS = HH // 2
    TURNS = TILES // UN

    with ExitStack() as ctx:
        def sb(name, shape, dt):
            return ctx.enter_context(nc.sbuf_tensor(n_ + name, shape, dt))

        ident = sb("ident", [P, P], F32)
        be_col = sb("be", [P, 1], F32)
        tie = sb("tie", [P, 1], F32)
        k_sb = sb("k", [P, HH, N], F32R)
        v_sb = sb("v", [P, HH, BLOCKS, E, PARTS, HD], BF16)
        q_sb = sb("q", [P, UN, HH, RPARTS, P], F32R)
        signs = sb("signs", [P, UN, N], I8)
        bias = sb("bias", [P, UN, N], BF16)
        scores = sb("scores", [P, 2 * CHUNKS - 1, SC], F32)
        top = sb("top", [P, 2, CHUNKS], F32)
        peaks = sb("peaks", [P, CHUNKS], F32)
        peak = sb("peak", [P, 1], F32)
        least = sb("least", [P, 1], F32)
        hits = sb("hits", [P, 2, N], F8)
        hitsT = sb("hitsT", [P, CHUNKS, TB, P, E], F8)
        xt = sb("xt", [P, UN, HALF], F32)
        picked = sb("picked", [P, 2, 2, PARTS, HD], F32)
        ps_s = ctx.enter_context(nc.psum_tensor(n_ + "ps_s", [P, max(PLACE) + 1, SC], F32))
        ps_t = ctx.enter_context(nc.psum_tensor(n_ + "ps_t", [P, 512], F32))
        ps_o = ctx.enter_context(nc.psum_tensor(n_ + "ps_o", [P, 512], F32))

        ident_ready = sem(n_ + "ident_ready")
        be_loaded = sem(n_ + "be_loaded")
        k_loaded = [[sem(n_ + f"k_loaded{h}_{c}") for c in range(CHUNKS)] for h in range(HH)]
        v_loaded = [sem(n_ + f"v_loaded{h}") for h in range(HH)]
        q_loaded = [sem(n_ + f"q_loaded{u}") for u in range(UN)]
        signs_ready = sem(n_ + "signs_ready")
        signs_stored = [sem(n_ + f"signs_stored{u}") for u in range(UN)]
        signs_loaded = [sem(n_ + f"signs_loaded{u}") for u in range(UN)]
        x_loaded = [sem(n_ + f"x_loaded{u}") for u in range(UN)]
        bias_ready = sem(n_ + "bias_ready")
        scores_ready = sem(n_ + "scores_ready")
        scores_used = sem(n_ + "scores_used")
        tie_ready = sem(n_ + "tie_ready")
        peak_ready = sem(n_ + "peak_ready")
        least_ready = sem(n_ + "least_ready")
        hits_ready = sem(n_ + "hits_ready")
        hits_turned = sem(n_ + "hits_turned")
        turned_kept = sem(n_ + "turned_kept")
        turned_used = sem(n_ + "turned_used")
        out_ready = sem(n_ + "out_ready")
        picked_ready = sem(n_ + "picked_ready")
        pool_step = sem(n_ + "pool_step")
        pair_added = sem(n_ + "pair_added")
        x1_stored = [sem(n_ + f"x1_stored{u}") for u in range(UN)]
        sp_passed = sem(n_ + "sp_passed")
        dve_passed = sem(n_ + "dve_passed")
        pe_passed = sem(n_ + "pe_passed")
        pool_passed = sem(n_ + "pool_passed")
        block = ctx.enter_context(nc.Block())

        @block.sync
        def _(sp):
            sp_gate = Gate(sp, sp_passed)
            sp.dma_start(be_col[:], be.rearrange("(a b) -> a b", a=1).broadcast_to([P, 1])).then_inc(be_loaded, 16)

            def load_k(half, h):
                for c in ORDER[h % 2]:
                    at = slice(c * SC, (c + 1) * SC)
                    sp.dma_start(k_sb[:, h, at].bitcast(F32), k_scr[half * HH + h, :, at]).then_inc(k_loaded[h][c], 16)

            def load_v(half, h):
                sp.dma_start(v_sb[:, h].rearrange("j b e c d -> j b (e c d)"), v_v[half * HH + h, :, :, :])\
                  .then_inc(v_loaded[h], 16)

            def load_q(half, t, u):
                for at in range(0, P, HD):
                    sp.dma_start(q_sb[at:at + HD, u, :, :, :].rearrange("p h s r -> p (h s) r").bitcast(F32),
                                 q_scr[half * HH:(half + 1) * HH, :, :, bass.ts(t, P)].rearrange("h s p r -> p (h s) r"))\
                      .then_inc(q_loaded[u], 16)

            def load_signs(t, u):
                sp.dma_start(signs[:, u, :], sign_scr[t, :, :]).then_inc(signs_loaded[u], 16)

            def load_adj(t):
                for i in range(2):
                    sp_gate.wait_ge(bias_ready, (t - 1) * 2 + (i + 1))
                    sp_gate.wait_ge(signs_ready, (t - 1) * 2 + (i + 1))
                    sp.dma_start(adj_rows[:, i, :], adj_v[t, :, i * HN:(i + 1) * HN]).then_inc(adj_loaded[i], 16)

            def store_signs(t, u):
                sp_gate.wait_ge(signs_ready, t * 2 + 2)
                sp.dma_start(sign_scr[t, :, :], signs[:, u, :]).then_inc(signs_stored[u], 16)

            def load_x(half, t, u):
                sp.dma_start(xt[:, u, :], x_v[t, :, half * HALF:(half + 1) * HALF]).then_inc(x_loaded[u], 16)

            def store(half, t, u):
                sp_gate.wait_ge(pair_added, (t + half * TILES) * PAIRS + (PAIRS + 2))
                sp.dma_start(x1_v[t, :, half * HALF:(half + 1) * HALF], xt[:, u, :]).then_inc(x1_stored[u], 16)

            def next_tile(half, t, u, stored_half, stored, turns):
                number = t + half * TILES
                if half == 0:
                    load_adj(t)
                    store_signs(t - 1, 1 - u)
                else:
                    sp_gate.wait_ge(bias_ready, (number - 1) * 2)
                    load_signs(t, u)
                sp_gate.wait_ge(scores_ready, (number - 1) * TILE_CHUNKS)
                load_q(half, t, u)
                store(stored_half, stored, u)
                sp_gate.wait_ge(x1_stored[u], turns * 16)
                load_x(half, t, u)

            load_q(0, 0, 0)
            for h in range(HH - 1):
                load_k(0, h)
            sp_gate.wait_ge(v_stored, GROUPS * GT * 16)
            load_v(0, 0)
            load_k(0, HH - 1)
            load_adj(1)
            store_signs(0, 0)
            load_v(0, 1)
            load_q(0, 1, 1)
            load_v(0, 2)
            load_x(0, 0, 0)
            load_v(0, 3)
            load_x(0, 1, 1)
            for half in range(HALVES):
                if half:
                    if half == 1:
                        store_signs(TILES - 1, 1)
                        for u in range(UN):
                            sp_gate.wait_ge(signs_stored[u], TURNS * 16)
                    sp_gate.wait_ge(bias_ready, (half * TILES - 1) * 2)
                    load_signs(0, 0)
                    sp_gate.wait_ge(scores_ready, (half * TILES - 1) * TILE_CHUNKS)
                    load_q(half, 0, 0)
                    for h in range(HH):
                        step = half * TILES * HH - HH + h
                        sp_gate.wait_ge(scores_ready, (step + 1) * CHUNKS)
                        load_k(half, h)
                        if h >= LAG:
                            sp_gate.wait_ge(turned_used, (step + 1 - LAG) * CHUNKS + 4)
                            load_v(half, h - LAG)
                        if h == 0:
                            store(half - 1, TILES - UN, 0)
                            sp_gate.wait_ge(x1_stored[0], half * (TILES // UN) * 16)
                            load_x(half, 0, 0)
                            sp_gate.wait_ge(bias_ready, half * TILES * 2)
                            load_signs(1, 1)
                    sp_gate.wait_ge(scores_ready, half * TILES * TILE_CHUNKS)
                    load_q(half, 1, 1)
                    for h in range(HH - LAG, HH):
                        sp_gate.wait_ge(turned_used, (half * TILES * HH - HH + h + 1) * CHUNKS + 4)
                        load_v(half, h)
                    store(half - 1, TILES - 1, 1)
                    sp_gate.wait_ge(x1_stored[1], half * (TILES // UN) * 16)
                    load_x(half, 1, 1)
                with sp.Fori(1, TILES // UN) as it:
                    for u in range(UN):
                        t = it * UN + u
                        next_tile(half, t, u, half, t - 2, it + half * (TILES // UN))
            for u in range(UN):
                store(HALVES - 1, TILES - UN + u, u)
            for u in range(UN):
                sp_gate.wait_ge(x1_stored[u], HALVES * (TILES // UN) * 16)

        @block.gpsimd
        def _(pool):
            make_identity(nc, pool, ident, ident_ready)
            pool.sem_inc(pair_added, 2)
            steps = Steps(pool, pool_step)
            gate = Gate(pool, pool_passed)

            def make_bias(number, u, turn, half):
                for i in range(2):
                    if half == 0:
                        source = adj_rows[:, i, :]
                        pool.wait_ge(adj_loaded[i], number * 16 + 16)
                    else:
                        source = signs[:, u, i * HN:(i + 1) * HN]
                        pool.wait_ge(signs_loaded[u], (turn - TURNS) * 16 + 16)
                    gate.wait_ge(scores_used, (number - 1) * TILE_CHUNKS)
                    nc.gpsimd.tensor_scalar(bias[:, u, i * HN:(i + 1) * HN], source, 0.0, MASKED, ALU.is_le, ALU.mult)\
                      .then_inc(bias_ready, 1)

            def add_pairs(number, u, turn):
                pool.wait_ge(x_loaded[u], turn * 16 + 16)
                steps.turn(number * (PAIRS * 2))
                for m in range(PAIRS):
                    pool.wait_ge(picked_ready, number * HH + (2 * m + 3))
                    part = [picked[:, m, :, n, :] for n in range(PARTS)]
                    to = xt[:, u, m * P:(m + 1) * P].rearrange("p (a d) -> p a d", a=2)
                    steps.done(nc.gpsimd.tensor_tensor(part[2], part[2], part[1], ALU.add))
                    steps.done(nc.gpsimd.tensor_tensor(part[2], part[2], part[0], ALU.add))
                    nc.gpsimd.tensor_tensor(to, to, part[2], ALU.add).then_inc(pair_added, 1)

            pool.wait_ge(bias_ready, UN * 2)
            for half in range(HALVES):
                with pool.Fori(max(1, half * TURNS), (half + 1) * TURNS) as it:
                    for u in range(UN):
                        make_bias(it * UN + u, u, it, half)
                        add_pairs(it * UN + (u - UN), u, it - 1)
            for u in range(UN):
                add_pairs(HALVES * TILES - UN + u, u, HALVES * TURNS - 1)

        @block.tensor
        def _(pe):
            gate = Gate(pe, pe_passed)
            pe.sem_inc(turned_used, 4)
            pe.wait_ge(ident_ready, 2)

            def score_chunk(s, j, i, it, new_half, first):
                u, h = j // HH % UN, j % HH
                if i == 0 and h == 0:
                    pe.wait_ge(q_loaded[u], it * 32 + 32)
                if not first or j > 0 or i == 3:
                    pe.wait_ge(scores_used, s * CHUNKS + (i + 1 - BACK[i]))
                c = ORDER[h % 2][i]
                if new_half:
                    pe.wait_ge(k_loaded[h][c], new_half * 16)
                for n in range(SC // 512):
                    keys = slice(c * SC + n * 512, c * SC + (n + 1) * 512)
                    for part in range(RPARTS):
                        last = nc.tensor.matmul(ps_s[:, PLACE[i], n * 512:(n + 1) * 512], q_sb[:, u, h, part, :],
                                                k_sb[:, h, keys], start=part == 0, stop=part == RPARTS - 1)
                last.then_inc(scores_ready, 1)

            def turn_chunk(s, h, c):
                if c == 0:
                    pe.wait_ge(hits_ready, s + 1)
                pe.wait_ge(turned_kept, s * CHUNKS + (c + 1))
                words = hits[:, h % 2, :].bitcast(F32)
                for b in range(TB):
                    at = (c * TB + b) * P
                    last = nc.tensor.transpose(ps_t[:, b * P:(b + 1) * P], words[:, at:at + P], ident[:])
                last.then_inc(hits_turned, 1)

            def value_chunk(s, h, c, new_half):
                if new_half and c == 0:
                    pe.wait_ge(v_loaded[h], new_half * 16)
                if c == 0:
                    gate.wait_ge(picked_ready, s + 1)
                if c == CHUNKS - 1:
                    gate.wait_ge(turned_kept, s * CHUNKS + (CHUNKS + 1))
                to = ps_o[:, 0:PARTS * HD].rearrange("p (c d) -> p c d", c=PARTS)
                for b in range(TB):
                    for e in range(E):
                        last = nc.tensor.matmul(to, hitsT[:, c, b, :, e],
                                                v_sb[:, h, c * TB + b, e, :, :],
                                                start=c == 0 and b == 0 and e == 0,
                                                stop=c == CHUNKS - 1 and b == TB - 1 and e == E - 1)
                last.then_inc(turned_used, 1)

            def turn(it, j, scored=True, turned=True, valued=True, half=-1, first=False):
                s = it * (UN * HH) + j
                new_keys = half + 1 if j < HH else 0
                new_values = half + 1 if LAG <= j < HH + LAG else 0
                for i in range(CHUNKS):
                    if scored:
                        score_chunk(s, j, i, it, new_keys, first)
                    if i == 0 and valued:
                        turn_chunk(s - LAG, (j - LAG) % HH, CHUNKS - 1)
                        for c in range(CHUNKS - 1):
                            value_chunk(s - LAG, (j - LAG) % HH, c, new_values)
                    if i > 0 and turned:
                        turn_chunk(s - TURN_LAG, (j - TURN_LAG) % HH, i - 1)
                    if i == 2 and valued:
                        value_chunk(s - LAG, (j - LAG) % HH, CHUNKS - 1, new_values)

            for half in range(HALVES):
                for j in range(UN * HH):
                    later = half > 0
                    turn(half * TURNS, j, True, later or j >= TURN_LAG, later or j >= LAG, half, not later)
                with pe.Fori(half * TURNS + 1, (half + 1) * TURNS) as it:
                    for j in range(UN * HH):
                        turn(it, j)
            for j in range(LAG):
                turn(HALVES * TURNS, j, False, j < TURN_LAG, True)

        @block.scalar
        def _(act):
            act.sem_inc(turned_kept, 1)
            act.sem_inc(picked_ready, 1)

            def make_signs(t, u, turn, i):
                act.wait_ge(adj_loaded[i], t * 16 + 16)
                if not isinstance(turn, int) or turn > 0:
                    act.wait_ge(signs_stored[u], turn * 16)
                nc.scalar.activation(signs[:, u, i * HN:(i + 1) * HN], adj_rows[:, i, :], ACT.Sign)\
                  .then_inc(signs_ready, 1)

            def find_least(s):
                act.wait_ge(peak_ready, s + 1)
                nc.scalar.activation(least[:], peak[:], ACT.Identity, bias=tie[:, 0:1], scale=1.0)\
                  .then_inc(least_ready, 1)

            def pick(s, pair, h):
                act.wait_ge(turned_used, s * CHUNKS + (CHUNKS + 4))
                if h % 2 == 0:
                    act.wait_ge(pair_added, pair + 1)
                nc.scalar.mul(picked[:, h // 2, h % 2, :, :].rearrange("p c d -> p (c d)"),
                              ps_o[:, 0:PARTS * HD], 1.0 / HEADS).then_inc(picked_ready, 1)

            def turn(it, signs_of=(), first=False, last=False):
                for j in range(UN * HH):
                    s = it * (UN * HH) + j
                    if not last or j < UN * HH - 1:
                        find_least(s + 1)
                    for c in range(CHUNKS):
                        act.wait_ge(hits_turned, s * CHUNKS + (c + 1))
                        act.wait_ge(turned_used, s * CHUNKS + (c + 1))
                        nc.scalar.copy(hitsT[:, c, :, :, :].rearrange("p b q e -> p (b q e)").bitcast(U16),
                                       ps_t[:, 0:TB * P].bitcast(U16)).then_inc(turned_kept, 1)
                        if c == 1 and (not first or j > 0):
                            pick(s - 1, it * (UN * PAIRS) + (j - 1) // 2, (j - 1) % HH)
                    if j // HH in signs_of and j % HH < 2:
                        nxt = j // HH + 1
                        make_signs(it * UN + nxt, nxt % UN, it + nxt // UN, j % HH)

            for i in range(2):
                make_signs(0, 0, 0, i)
            act.wait_ge(tie_ready, 1)
            find_least(0)
            turn(0, range(UN), first=True)
            with act.Fori(1, TURNS - 1) as it:
                turn(it, range(UN))
            turn(TURNS - 1, range(UN - 1))
            with act.Fori(TURNS, HALVES * TURNS - 1) as it:
                turn(it)
            turn(HALVES * TURNS - 1, last=True)
            pick(HALVES * TILES * HH - 1, HALVES * TILES * PAIRS - 1, HH - 1)

        @block.vector
        def _(v):
            gate = Gate(v, dve_passed)

            def make_bias(t):
                for i in range(2):
                    v.wait_ge(adj_loaded[i], t * 16 + 16)
                    nc.vector.tensor_scalar(bias[:, t, i * HN:(i + 1) * HN], adj_rows[:, i, :], 0.0, MASKED,
                                            ALU.is_le, ALU.mult).then_inc(bias_ready, 1)

            nc.vector.memset(tie[:], -TIE).then_inc(tie_ready, 1)
            make_bias(0)
            v.wait_ge(be_loaded, 16)

            def mask_chunk(s, j, i):
                gate.wait_ge(scores_ready, s * CHUNKS + (i + 1))
                c = ORDER[j % 2][i]
                nc.vector.tensor_tensor_reduce(scores[:, (CHUNKS - 1) * (j % 2) + c, :], ps_s[:, PLACE[i], :],
                                               bias[:, j // HH, c * SC:(c + 1) * SC], 1.0, FLOOR,
                                               ALU.add, ALU.max, top[:, j % 2, c:c + 1]).then_inc(scores_used, 1)

            def find_peak(s, a):
                gate.wait_ge(scores_used, s * CHUNKS + CHUNKS)
                nc.vector.tensor_tensor_reduce(peaks[:], top[:, a, :], be_col[:].broadcast_to([P, CHUNKS]), 1.0,
                                               LOWEST, ALU.add, ALU.max, peak[:])\
                  .then_inc(peak_ready, 1)

            def compare(s, a, reused):
                gate.wait_ge(least_ready, s + 1)
                if reused:
                    gate.wait_ge(hits_turned, (s - 1) * CHUNKS)
                at = (CHUNKS - 1) * a
                nc.vector.tensor_scalar(hits[:, a, :], scores[:, at:at + CHUNKS, :].rearrange("p c k -> p (c k)"),
                                        be_col[:, 0:1], least[:, 0:1], ALU.add, ALU.is_ge, saturate=False)\
                  .then_inc(hits_ready, 1)

            def turn(it, first):
                for j in range(UN * HH):
                    s = it * (UN * HH) + j
                    if first and j == HH:
                        make_bias(1)
                    if j % HH == 0:
                        v.wait_ge(bias_ready, (it * UN + j // HH) * 2 + 2)
                    mask_chunk(s, j, 0)
                    if not first or j > 0:
                        find_peak(s - 1, (j - 1) % 2)
                    mask_chunk(s, j, 1)
                    if not first or j > 0:
                        compare(s - 1, (j - 1) % 2, not first or j > 2)
                    mask_chunk(s, j, 2)
                    if not first or j > 0:
                        gate.wait_ge(hits_ready, s)
                    mask_chunk(s, j, 3)

            turn(0, True)
            with v.Fori(1, HALVES * TURNS) as it:
                turn(it, False)
            last = HALVES * TILES * HH - 1
            find_peak(last, 1)
            compare(last, 1, True)


def layer1(nc, sem, adj_signs, x1_scr, u_scr, W_self, b_self, W_nb, b_nb, W_comb, b_comb, out):
    with ExitStack() as outer:
        g_sb = outer.enter_context(nc.sbuf_tensor("g_parts", [P, TILES, RPARTS, D], F32R))
        ident = outer.enter_context(nc.sbuf_tensor("l_ident", [P, P], F32))
        with ExitStack() as maps:
            w = maps.enter_context(nc.sbuf_tensor("l_w", [P, 2, RPARTS, KC, D], F32R))
            b_row = maps.enter_context(nc.sbuf_tensor("l_b_row", [P, D], F32))
            xb = maps.enter_context(nc.sbuf_tensor("l_x", [P, 2, GT, D], F32))
            x_loaded = [sem(f"l_x_loaded{u}") for u in range(2)]
            norm_buffers = [maps.enter_context(nc.sbuf_tensor(f"l_{name}", shape, F32)) for name, shape in
                            (("xn", [P, GT, D]), ("stats", [P, GT, 6]), ("mv", [P, GT, 2]), ("small", [P, 4, GT]))]
            norm_sems = [sem(f"l_{name}") for name in ("var_ready", "root_ready", "xn_ready", "norm_step")]
            multiply_weights(nc, sem, x1_scr, ident, w, b_row, xb, x_loaded, norm_buffers, norm_sems,
                             W_self, b_self, W_nb, b_nb, W_comb, b_comb)
            linear_maps(nc, sem, x1_scr, u_scr, g_sb, ident, w, b_row, xb, x_loaded, norm_buffers, norm_sems)
        aggregation(nc, sem, x1_scr, adj_signs, u_scr, g_sb, ident, out)


def group_rows(scr):
    return scr.rearrange("(g j e) f -> g j (e f)", j=P, e=E)


def multiply_weights(nc, sem, x1_scr, ident, w, b_row, xb, x_loaded, norm_buffers, norm_sems,
                     W_self, b_self, W_nb, b_nb, W_comb, b_comb):
    xn, stats, mv, small = norm_buffers
    var_ready, root_ready, xn_ready, norm_step = norm_sems
    with ExitStack() as ctx:
        def sb(name, shape, dt):
            return ctx.enter_context(nc.sbuf_tensor(name, shape, dt))

        w_rows = sb("w_rows", [P, KC, D], F32)
        w_rowsT = sb("w_rowsT", [P, KC, D], F32)
        combs = (xn, xb[:, 1])
        b_cols = sb("w_b_cols", [P, 2 * KC], F32)
        b_wide = sb("w_b_wide", [P, 2 * KC, P], F32)
        ones = sb("w_ones", [P, P], F32)
        ps_t = ctx.enter_context(nc.psum_tensor("w_ps_t", [P, 2, D], F32))
        ps_o = ctx.enter_context(nc.psum_tensor("w_ps_o", [P, KC, D], F32))
        ps_b = ctx.enter_context(nc.psum_tensor("w_ps_b", [P, D], F32))

        ident_ready = sem("w_ident_ready")
        rows_loaded = [sem(f"w_rows_loaded{i}") for i in range(2)]
        comb_loaded = [sem(f"w_comb_loaded{i}") for i in range(2)]
        dve_passed = sem("w_dve_passed")
        b_loaded = sem("w_b_loaded")
        ones_ready = sem("w_ones_ready")
        wide_ready = sem("w_wide_ready")
        bias_ready = sem("w_bias_ready")
        rows_turned = sem("w_rows_turned")
        turned_kept = sem("w_turned_kept")
        w_ready = sem("w_w_ready")
        high_ready = sem("w_high_ready")
        low_ready = sem("w_low_ready")
        block = ctx.enter_context(nc.Block())

        @block.gpsimd
        def _(pool):
            make_identity(nc, pool, ident, ident_ready)

        @block.sync
        def _(sp):
            def load_w(to, w, loaded):
                sp.dma_start(to, w.rearrange("(c p) f -> p c f", p=P)).then_inc(loaded, 16)

            load_w(w_rows[:], W_self, rows_loaded[0])
            load_w(combs[0][:], W_comb[0:D, :], comb_loaded[0])
            for i, b in enumerate((b_self, b_nb)):
                sp.dma_start(b_cols[:, i * KC:(i + 1) * KC], b.rearrange("(c p) -> p c", p=P),
                             allow_slow_non_contiguous=True).then_inc(b_loaded, 16)
            sp.dma_start(b_row[:], b_comb.rearrange("(a f) -> a f", a=1).broadcast_to([P, D])).then_inc(b_loaded, 16)
            load_w(combs[1], W_comb[D:2 * D, :], comb_loaded[1])
            sp.wait_ge(rows_turned, KC)
            load_w(w_rows[:], W_nb, rows_loaded[1])
            sp.dma_start(xb[:, 0, :, :].rearrange("j e f -> j (e f)"), group_rows(x1_scr)[0, :, :])\
              .then_inc(x_loaded[0], 16)

        @block.tensor
        def _(pe):
            pe.wait_ge(ident_ready, 2)
            for i, comb in enumerate(combs):
                pe.wait_ge(rows_loaded[i], 16)
                for k in range(KC):
                    f = i * KC + k
                    pe.wait_ge(turned_kept, f + 1)
                    for c in range(KC):
                        last = nc.tensor.transpose(ps_t[:, f % 2, c * P:(c + 1) * P],
                                                   w_rows[:, c, k * P:(k + 1) * P], ident[:])
                    last.then_inc(rows_turned, 1)
                pe.wait_ge(comb_loaded[i], 16)
                if i == 0:
                    pe.wait_ge(wide_ready, 2 * KC)
                for k in range(KC):
                    last = nc.tensor.matmul(ps_b[:], b_wide[:, i * KC + k, :], comb[:, k, :],
                                            start=i == 0 and k == 0, stop=i == 1 and k == KC - 1,
                                            skip_group_check=True)
                if i == 1:
                    last.then_inc(bias_ready, 1)
                pe.wait_ge(turned_kept, i * KC + KC + 2)
                for c in range(KC):
                    if i == 1:
                        pe.wait_ge(low_ready, c + 1)
                    for k in range(KC):
                        last = nc.tensor.matmul(ps_o[:, c, :], w_rowsT[:, k, c * P:(c + 1) * P], comb[:, k, :],
                                                start=k == 0, stop=k == KC - 1)
                    last.then_inc(w_ready, 1)

        @block.scalar
        def _(act):
            act.sem_inc(turned_kept, 2)
            for i in range(2):
                if i == 1:
                    act.wait_ge(w_ready, KC)
                for k in range(KC):
                    f = i * KC + k
                    act.wait_ge(rows_turned, f + 1)
                    nc.scalar.copy(w_rowsT[:, k, :], ps_t[:, f % 2, :]).then_inc(turned_kept, 1)
                if i == 1:
                    act.wait_ge(var_ready, 1)
                    nc.scalar.activation(small[:, 1, :], small[:, 0, :], ACT.Sqrt).then_inc(root_ready, 1)
                for c in range(KC):
                    act.wait_ge(w_ready, i * KC + c + 1)
                    nc.scalar.copy(w[:, i, 0, c, :], ps_o[:, c, :]).then_inc(high_ready, 1)

        @block.vector
        def _(v):
            nc.vector.memset(ones[:], 1.0).then_inc(ones_ready, 1)
            v.wait_ge(ones_ready, 1)
            v.wait_ge(b_loaded, 3 * 16)
            for c in range(2 * KC):
                nc.vector.tensor_scalar(b_wide[:, c, :], ones[:], b_cols[:, c:c + 1], None, ALU.mult)\
                  .then_inc(wide_ready, 1)
            for i in range(2):
                if i == 1:
                    v.wait_ge(x_loaded[0], 16)
                    v.wait_ge(w_ready, KC)
                    normalise(nc, v, Gate(v, dve_passed), Steps(v, norm_step), xb[:, 0], xn, stats, mv, small,
                              var_ready, root_ready, 0).then_inc(xn_ready, 1)
                for c in range(KC):
                    v.wait_ge(high_ready, i * KC + c + 1)
                    nc.vector.tensor_tensor(w[:, i, 1, c, :], ps_o[:, c, :], w[:, i, 0, c, :].bitcast(F32),
                                            ALU.subtract).then_inc(low_ready, 1)
            v.wait_ge(bias_ready, 1)
            nc.vector.tensor_tensor(b_row[:], ps_b[:], b_row[:], ALU.add)


def linear_maps(nc, sem, x1_scr, u_scr, g_sb, ident, w, b_row, xb, x_loaded, norm_buffers, norm_sems):
    xn, stats, mv, small = norm_buffers
    var_ready, root_ready, xn_ready, norm_step = norm_sems
    UN = 2
    OUTS = 2 * GT
    assert GT == E
    x1_g = group_rows(x1_scr)
    u_v = u_scr.rearrange("(g j e) f -> g e j f", j=P, e=E)
    PRODUCTS = ((0, 0), (0, 1), (1, 0))
    TURNED_AT = {0: ((0, 2), (0, 3)), 2: ((1, 0), (1, 1))}
    with ExitStack() as ctx:
        def sb(name, shape, dt):
            return ctx.enter_context(nc.sbuf_tensor(name, shape, dt))

        hT = sb("l_hT", [P, GT, RPARTS, KC, P], F32R)
        u_sb = sb("l_u", [P, 2, D], F32)
        ps_t = ctx.enter_context(nc.psum_tensor("l_ps_t", [P, 2, D], F32))
        ps_o = ctx.enter_context(nc.psum_tensor("l_ps_o", [P, 4, D], F32))

        tile_turned = sem("l_tile_turned")
        turned_high = sem("l_turned_high")
        turned_kept = sem("l_turned_kept")
        out_ready = sem("l_out_ready")
        high_ready = sem("l_high_ready")
        u_ready = sem("l_u_ready")
        low_ready = sem("l_low_ready")
        u_stored = [sem(f"l_u_stored{a}") for a in range(2)]
        sp_passed = sem("l_sp_passed")
        dve_passed = sem("l_dve_passed")
        block = ctx.enter_context(nc.Block())

        def g_part(tile, part):
            return g_sb[:, bass.ds(tile, 1), part, :].rearrange("p a f -> p (a f)")

        @block.sync
        def _(sp):
            sp_gate = Gate(sp, sp_passed)

            def load_x(g, u):
                sp.dma_start(xb[:, u, :, :].rearrange("j e f -> j (e f)"), x1_g[g, :, :]).then_inc(x_loaded[u], 16)

            def group(g, u, last):
                if not last:
                    sp_gate.wait_ge(xn_ready, g + 1)
                    load_x(g + 2, u)
                for t in range(GT):
                    sp_gate.wait_ge(u_ready, g * GT + (t + 1))
                    sp.dma_start(u_v[g, t, :, :], u_sb[:, t % 2, :]).then_inc(u_stored[t % 2], 16)

            load_x(1, 1)
            with sp.Fori(0, GROUPS // UN - 1) as it:
                for u in range(UN):
                    group(it * UN + u, u, False)
            for u in range(UN):
                group(GROUPS - UN + u, u, True)
            for a in range(2):
                sp_gate.wait_ge(u_stored[a], TILES // 2 * 16)

        @block.tensor
        def _(pe):
            def turn_tile(g, t):
                if t == 0:
                    pe.wait_ge(xn_ready, g + 1)
                pe.wait_ge(turned_kept, g * GT + (t + 1))
                for k in range(KC):
                    last = nc.tensor.transpose(ps_t[:, t % 2, k * P:(k + 1) * P],
                                               xn[:, t, k * P:(k + 1) * P], ident[:])
                last.then_inc(tile_turned, 1)

            def group(g, last_group=False):
                for t in range(GT):
                    pe.wait_ge(turned_kept, g * GT + (t + 3))
                    for i in range(2):
                        if t >= 2 or not isinstance(g, int) or g > 0:
                            pe.wait_ge((u_ready, low_ready)[i], g * GT + (t - 1))
                        for k in range(KC):
                            for n, (a, b) in enumerate(PRODUCTS):
                                last = nc.tensor.matmul(ps_o[:, 2 * (t % 2) + i, :], hT[:, t, a, k, :], w[:, i, b, k, :],
                                                        start=k == 0 and n == 0,
                                                        stop=k == KC - 1 and n == len(PRODUCTS) - 1)
                        last.then_inc(out_ready, 1)
                    for later, tile in TURNED_AT.get(t, ()):
                        if not (later and last_group):
                            turn_tile(g + later, tile)

            for t in range(2):
                turn_tile(0, t)
            group(0)
            group(1)
            with pe.Fori(1, GROUPS // UN - 1) as it:
                for u in range(UN):
                    group(it * UN + u)
            for u in range(UN):
                group(GROUPS - UN + u, u == UN - 1)

        @block.scalar
        def _(act):
            def root(g):
                act.wait_ge(var_ready, g + 1)
                nc.scalar.activation(small[:, 1, :], small[:, 0, :], ACT.Sqrt).then_inc(root_ready, 1)

            def keep_tile(g, t):
                act.wait_ge(tile_turned, g * GT + (t + 1))
                nc.scalar.activation(hT[:, t, 0, :, :].rearrange("p k r -> p (k r)"), ps_t[:, t % 2, :], ACT.Relu)\
                  .then_inc(turned_high, 1)

            def group(g, last_group=False):
                for t in range(GT):
                    act.wait_ge(out_ready, g * OUTS + (2 * t + 2))
                    nc.scalar.copy(g_part(g * GT + t, 0), ps_o[:, 2 * (t % 2) + 1, :]).then_inc(high_ready, 1)
                    for later, tile in TURNED_AT.get(t, ()):
                        if not (later and last_group):
                            keep_tile(g + later, tile)
                    if t == 0 and not last_group:
                        root(g + 1)

            for t in range(2):
                keep_tile(0, t)
            group(0)
            group(1)
            with act.Fori(1, GROUPS // UN - 1) as it:
                for u in range(UN):
                    group(it * UN + u)
            for u in range(UN):
                group(GROUPS - UN + u, u == UN - 1)

        @block.vector
        def _(v):
            v.sem_inc(turned_kept, 2)
            steps = Steps(v, norm_step)
            NORM = NORM_STEPS - 2

            def norm(g, u, it):
                v.wait_ge(x_loaded[u], it * 16 + 16)
                v.wait_ge(turned_kept, g * GT + 2)
                steps.turn(g * NORM)
                normalise(nc, v, Gate(v, dve_passed), steps, xb[:, u], xn, stats, mv, small, var_ready, root_ready, g)\
                    .then_inc(xn_ready, 1)
                assert steps.n == NORM, steps.n

            def keep_tile(g, t):
                v.wait_ge(turned_high, g * GT + (t + 1))
                nc.vector.scalar_tensor_tensor(hT[:, t, 1, :, :].rearrange("p k r -> p (k r)"), ps_t[:, t % 2, :], 0.0,
                                               hT[:, t, 0, :, :].rearrange("p k r -> p (k r)").bitcast(F32),
                                               ALU.max, ALU.subtract).then_inc(turned_kept, 1)

            def group(g, u, it, last_group=False):
                for t in range(GT):
                    v.wait_ge(out_ready, g * OUTS + (2 * t + 1))
                    if not isinstance(g, int) or g * GT + t >= 2:
                        v.wait_ge(u_stored[t % 2], (g * 2 + t // 2) * 16)
                    nc.vector.tensor_tensor(u_sb[:, t % 2, :], ps_o[:, 2 * (t % 2), :], b_row[:], ALU.add)\
                      .then_inc(u_ready, 1)
                    v.wait_ge(high_ready, g * GT + (t + 1))
                    nc.vector.tensor_tensor(g_part(g * GT + t, 1), ps_o[:, 2 * (t % 2) + 1, :],
                                            g_part(g * GT + t, 0).bitcast(F32), ALU.subtract).then_inc(low_ready, 1)
                    for later, tile in TURNED_AT.get(t, ()):
                        if not (later and last_group):
                            keep_tile(g + later, tile)
                    if t == 0 and not last_group:
                        norm(g + 1, 1 - u, it + u)

            for t in range(2):
                keep_tile(0, t)
            group(0, 0, 0)
            group(1, 1, 0)
            with v.Fori(1, GROUPS // UN - 1) as it:
                for u in range(UN):
                    group(it * UN + u, u, it)
            for u in range(UN):
                group(GROUPS - UN + u, u, GROUPS // UN - 1, u == UN - 1)


def aggregation(nc, sem, x1_scr, sign_scr, u_scr, g_sb, ident, out):
    UN = 2
    x1_v, u_v, out_v = (a.rearrange("(b u p) f -> b u p f", u=UN, p=P) for a in (x1_scr, u_scr, out))
    sign_v = sign_scr.rearrange("(b u) p k -> b u p k", u=UN)
    with ExitStack() as ctx:
        def sb(name, shape, dt):
            return ctx.enter_context(nc.sbuf_tensor(name, shape, dt))

        signs = sb("g_signs", [P, UN, N], I8)
        mask = sb("g_mask", [P, UN, N], F8)
        maskT = sb("g_maskT", [P, UN, BLOCKS, E, P], F32R)
        deg = sb("g_deg", [P, UN, 3], F32)
        u_sb = sb("g_u", [P, UN, D], F32)
        x1 = sb("g_x1", [P, UN, D], F32)
        mixed = sb("g_mixed", [P, D], F32)
        y = sb("g_y", [P, UN, D], F32)
        ps_t = ctx.enter_context(nc.psum_tensor("g_ps_t", [P, 2, 512], F32))
        ps_o = ctx.enter_context(nc.psum_tensor("g_ps_o", [P, 2, D], F32))

        signs_loaded = [sem(f"g_signs_loaded{u}") for u in range(UN)]
        rows_loaded = [sem(f"g_rows_loaded{u}") for u in range(UN)]
        mask_ready = sem("g_mask_ready")
        deg_ready = sem("g_deg_ready")
        mask_turned = sem("g_mask_turned")
        turned_kept = sem("g_turned_kept")
        sum_ready = sem("g_sum_ready")
        sum_used = sem("g_sum_used")
        y_ready = sem("g_y_ready")
        y_stored = [sem(f"g_y_stored{u}") for u in range(UN)]
        sp_passed = sem("g_sp_passed")
        dve_passed = sem("g_dve_passed")
        pe_passed = sem("g_pe_passed")
        act_passed = sem("g_act_passed")
        block = ctx.enter_context(nc.Block())

        @block.sync
        def _(sp):
            sp_gate = Gate(sp, sp_passed)
            def load_signs(b, u):
                sp.dma_start(signs[:, u, :], sign_v[b, u, :, :]).then_inc(signs_loaded[u], 16)

            def load_rows(b, u):
                sp.dma_start(u_sb[:, u, :], u_v[b, u, :, :]).then_inc(rows_loaded[u], 16)
                sp.dma_start(x1[:, u, :], x1_v[b, u, :, :]).then_inc(rows_loaded[u], 16)

            def store(b, u):
                sp_gate.wait_ge(y_ready, b * 2 + (u + 1))
                sp.dma_start(out_v[b, u, :, :], y[:, u, :]).then_inc(y_stored[u], 16)

            for u in range(UN):
                load_signs(0, u)
            for u in range(UN):
                load_rows(0, u)
            with sp.Fori(1, TILES // UN) as b:
                for u in range(UN):
                    sp_gate.wait_ge(mask_ready, b * 2 + (u - 1))
                    load_signs(b, u)
                    store(b - 1, u)
                    load_rows(b, u)
            for u in range(UN):
                store(TILES // UN - 1, u)
            for u in range(UN):
                sp_gate.wait_ge(y_stored[u], TILES // UN * 16)

        @block.tensor
        def _(pe):
            gate = Gate(pe, pe_passed)

            def turn_chunk(n, u, c):
                if c == 0:
                    pe.wait_ge(mask_ready, n + 1)
                pe.wait_ge(turned_kept, n * CHUNKS + (c + 1))
                words = mask[:, u, :].bitcast(F32)
                for b in range(TB):
                    at = (c * TB + b) * P
                    last = nc.tensor.transpose(ps_t[:, c % 2, b * P:(b + 1) * P], words[:, at:at + P], ident[:])
                last.then_inc(mask_turned, 1)

            def sum_chunk(n, u, c):
                if c == 0:
                    pe.wait_ge(sum_used, n + 1)
                    gate.wait_ge(turned_kept, n * CHUNKS + (CHUNKS + 2))
                for b in range(c * TB, (c + 1) * TB):
                    for e in range(E):
                        for part in range(RPARTS):
                            last = nc.tensor.matmul(ps_o[:, u, :], maskT[:, u, b, e, :], g_sb[:, E * b + e, part, :],
                                                    start=b == 0 and e == 0 and part == 0,
                                                    stop=b == BLOCKS - 1 and e == E - 1 and part == RPARTS - 1)
                if c == CHUNKS - 1:
                    last.then_inc(sum_ready, 1)

            def tile(n, u, last):
                for c in range(CHUNKS):
                    sum_chunk(n, u, c)
                    if not last and c < CHUNKS - 1:
                        turn_chunk(n + 1, 1 - u, c)
                        if c == CHUNKS - 2:
                            turn_chunk(n + 1, 1 - u, CHUNKS - 1)

            for c in range(CHUNKS):
                turn_chunk(0, 0, c)
            with pe.Fori(0, TILES // UN - 1) as b:
                for u in range(UN):
                    tile(b * 2 + u, u, False)
            for u in range(UN):
                tile(TILES - UN + u, u, u == UN - 1)

        @block.scalar
        def _(act):
            act.sem_inc(turned_kept, 2)
            act_gate = Gate(act, act_passed)

            def keep(n, u, b):
                if not isinstance(b, int) or b > 0:
                    act.wait_ge(sum_ready, n - 1)
                for c in range(CHUNKS):
                    act_gate.wait_ge(mask_turned, n * CHUNKS + (c + 1))
                    nc.scalar.copy(maskT[:, u, c * TB:(c + 1) * TB, :, :].rearrange("p b e q -> p b q e"),
                                   ps_t[:, c % 2, 0:TB * P].bitcast(F8).rearrange("p (b q e) -> p b q e", q=P, e=E))\
                      .then_inc(turned_kept, 1)

            for u in range(UN):
                keep(u, u, 0)
            with act.Fori(1, TILES // UN) as b:
                for u in range(UN):
                    keep(b * 2 + u, u, b)

        @block.vector
        def _(v):
            v.sem_inc(sum_used, 2)
            gate = Gate(v, dve_passed)

            def masks(n, u, b):
                v.wait_ge(signs_loaded[u], b * 16 + 16)
                if not isinstance(n, int) or n >= 2:
                    gate.wait_ge(mask_turned, (n - 1) * CHUNKS)
                nc.vector.tensor_scalar(mask[:, u, :], signs[:, u, :], 0.0, 0.0, ALU.is_gt, ALU.add,
                                        accum_out=deg[:, u, 0:1], saturate=False).then_inc(mask_ready, 1)

            def inverse(n, u):
                v.wait_ge(mask_ready, n + 1)
                nc.vector.tensor_scalar(deg[:, u, 1:2], deg[:, u, 0:1], 1.0, None, ALU.max).then_inc(deg_ready, 1)
                v.wait_ge(deg_ready, n * 2 + 1)
                nc.vector.reciprocal(deg[:, u, 2:3], deg[:, u, 1:2]).then_inc(deg_ready, 1)

            def finish(n, u, b):
                if not isinstance(n, int) or n > 0:
                    v.wait_ge(y_ready, n)
                v.wait_ge(sum_ready, n + 1)
                v.wait_ge(rows_loaded[u], b * 32 + 32)
                v.wait_ge(deg_ready, n * 2 + 2)
                nc.vector.scalar_tensor_tensor(mixed[:], ps_o[:, u, :], deg[:, u, 2:3], u_sb[:, u, :],
                                               ALU.mult, ALU.add).then_inc(sum_used, 1)
                v.wait_ge(sum_used, n + 3)
                if not isinstance(b, int) or b > 0:
                    v.wait_ge(y_stored[u], b * 16)
                nc.vector.scalar_tensor_tensor(y[:, u, :], mixed[:], 0.0, x1[:, u, :],
                                               ALU.max, ALU.add).then_inc(y_ready, 1)

            def turn(b):
                for u in range(UN):
                    masks(b * 2 + (u + 2), u, b + 1)
                    finish(b * 2 + u, u, b)
                    inverse(b * 2 + (u + 2), u)

            for u in range(UN):
                masks(u, u, 0)
                inverse(u, u)
            turn(0)
            with v.Fori(1, TILES // UN - 1) as b:
                turn(b)
            for u in range(UN):
                finish(TILES - UN + u, u, TILES // UN - 1)


def two_layers(nc, x, adj, WQ, WK, WV, we, be, W_self, b_self, W_nb, b_nb, W_comb, b_comb, out):
    def scratch(name, shape, dt):
        return nc.dram_tensor(name, shape, dt).ap()

    q_scr = scratch("q_scr", [HEADS, RPARTS, HD, N], F32)
    k_scr = scratch("k_scr", [HEADS, RPARTS * HD, N], F32)
    v_scr = scratch("v_scr", [HEADS, N, PARTS, HD], BF16)
    sign_scr = scratch("sign_scr", [TILES, P, N], I8)
    x1_scr = scratch("x1_scr", [N, D], F32)
    u_scr = scratch("u_scr", [N, D], F32)
    with ExitStack() as sems:
        def sem(name):
            return sems.enter_context(nc.semaphore(name))

        v_stored = sem("v_stored")
        adj_loaded = [sem(f"adj_loaded{i}") for i in range(2)]
        with nc.sbuf_tensor("adj_rows", [P, 2, HN], I32) as adj_rows:
            projections(nc, sem, x, WQ, WK, WV, we, q_scr, k_scr, v_scr, v_stored, adj, adj_rows, adj_loaded)
            attention(nc, sem, x, adj, adj_rows, adj_loaded, be, q_scr, k_scr, v_scr, v_stored, sign_scr, x1_scr)
        layer1(nc, sem, sign_scr, x1_scr, u_scr, W_self, b_self, W_nb, b_nb, W_comb, b_comb, out)


_INS = ["x", "adj", "L0_gnn_WQ", "L0_gnn_WK", "L0_gnn_WV", "L0_gnn_we", "L0_gnn_be",
        "L1_gnn_W_self", "L1_gnn_b_self", "L1_gnn_W_nb", "L1_gnn_b_nb", "L1_gnn_W_comb", "L1_gnn_b_comb"]


def kernel(**inputs):
    import numpy as _np
    import concourse.bacc as _bacc
    from concourse import mybir as _mybir
    from concourse.bass_utils import run_bass_kernel_spmd as _run

    nc = _bacc.Bacc("TRN2", target_bir_lowering=False, num_devices=1)
    arrays, args = {}, []
    for name in _INS:
        a = _np.ascontiguousarray(inputs[name])
        arrays[f"in_{name}_dram"] = a
        args.append(nc.dram_tensor(f"in_{name}_dram", a.shape, _mybir.dt.from_np(a.dtype), kind="ExternalInput").ap())
    args.append(nc.dram_tensor("out_0_dram", (N, D), F32, kind="ExternalOutput").ap())
    two_layers(nc, *args)
    r = _run(nc, [arrays], core_ids=[0])
    return r.results[0]["out_0_dram"]
```
